# Optimizing a Trainium2 kernel written in Bass

```python
import numpy as np
import jax
import jax.numpy as jnp

def _softmax(x, axis=-1):
    return jax.nn.softmax(x, axis=axis)

def _gelu(x):
    return jax.nn.gelu(x, approximate=True)

def _silu(x):
    return jax.nn.silu(x)

def _sigmoid(x):
    return jax.nn.sigmoid(x)

def _layernorm(x, axis=-1, eps=1e-05):
    m = jnp.mean(x, axis=axis, keepdims=True)
    v = jnp.var(x, axis=axis, keepdims=True)
    return (x - m) / jnp.sqrt(v + eps)

def _scatter_add(tgt, idx, src, axis=0):
    return tgt.at[idx].add(src)

def _segment_sum(src, seg, n):
    return jax.ops.segment_sum(src, seg, n)
kernel_name = 'mk_sandwich_d1_jaxref_r8_5de0bf'

def setup_inputs(seed: int=0):
    np.random.seed(seed)
    _w = jnp.asarray

    def _L0_attn_setup():
        import jax, jax.numpy as jnp
        import numpy as np
        H = 16
        D = 64
        E = 128
        NEG_INF = float('-inf')

        def _layer_norm(x, g, b, eps=1e-05):
            mu = jnp.mean(x, axis=-1, keepdims=True)
            var = jnp.mean(jnp.square(x - mu), axis=-1, keepdims=True)
            return (x - mu) * jax.lax.rsqrt(var + eps) * g + b
        key = jax.random.key(seed)
        ks = jax.random.split(key, 10)
        B, S = (2, 256)
        sc_in = 1.0 / np.sqrt(E)
        sc_h = 1.0 / np.sqrt(H * D)
        return {'x': jax.random.normal(ks[0], (B, S, E), jnp.float32), 'ln_g': jnp.ones((E,), jnp.float32), 'ln_b': jnp.zeros((E,), jnp.float32), 'wq': jax.random.uniform(ks[1], (E, H * D), jnp.float32, -sc_in, sc_in), 'bq': jnp.zeros((H * D,), jnp.float32), 'wk': jax.random.uniform(ks[2], (E, H * D), jnp.float32, -sc_in, sc_in), 'bk': jnp.zeros((H * D,), jnp.float32), 'wv': jax.random.uniform(ks[3], (E, H * D), jnp.float32, -sc_in, sc_in), 'bv': jnp.zeros((H * D,), jnp.float32), 'w0': jax.random.uniform(ks[4], (H * D, E), jnp.float32, -sc_h, sc_h), 'b0': jnp.zeros((E,), jnp.float32)}
    _L0_attn_in = _L0_attn_setup()

    def _L0_ffn_setup():
        import jax, jax.numpy as jnp
        import numpy as np
        B, L, H = (32, 64, 128)
        E, R, TOP_K = (8, 16, 2)

        def _gates(cls, router_w):
            logits = jnp.einsum('bh,eh->be', cls, router_w)
            top_vals, top_idx = jax.lax.top_k(logits, TOP_K)
            mask = jnp.full_like(logits, -jnp.inf)
            rows = jnp.arange(logits.shape[0])[:, None]
            mask = mask.at[rows, top_idx].set(top_vals)
            return jax.nn.softmax(mask, axis=1)
        key = jax.random.key(seed)
        k1, k2, k3, k4 = jax.random.split(key, 4)
        x = jax.random.normal(k1, (B, L, H), dtype=jnp.float32)
        router_w = jax.random.normal(k2, (E, H), dtype=jnp.float32) * 0.02
        lora_down = jax.random.normal(k3, (E, R, H), dtype=jnp.float32) * (1.0 / np.sqrt(H))
        lora_up = jax.random.normal(k4, (E, H, R), dtype=jnp.float32) * (1.0 / np.sqrt(R))
        return {'x': x, 'router_w': router_w, 'lora_down': lora_down, 'lora_up': lora_up}
    _L0_ffn_in = _L0_ffn_setup()
    _d = {'L0_attn_x': _L0_attn_in['x'], 'L0_attn_ln_g': _L0_attn_in['ln_g'], 'L0_attn_ln_b': _L0_attn_in['ln_b'], 'L0_attn_wq': _L0_attn_in['wq'], 'L0_attn_bq': _L0_attn_in['bq'], 'L0_attn_wk': _L0_attn_in['wk'], 'L0_attn_bk': _L0_attn_in['bk'], 'L0_attn_wv': _L0_attn_in['wv'], 'L0_attn_bv': _L0_attn_in['bv'], 'L0_attn_w0': _L0_attn_in['w0'], 'L0_attn_b0': _L0_attn_in['b0'], 'L0_ffn_router_w': _L0_ffn_in['router_w'], 'L0_ffn_lora_down': _L0_ffn_in['lora_down'], 'L0_ffn_lora_up': _L0_ffn_in['lora_up']}
    _x0 = _d['L0_attn_x']
    _d['L0_attn_x'] = jax.random.normal(jax.random.fold_in(jax.random.key(seed), 1), (4, 1024, 128), dtype=_x0.dtype)
    del _x0
    return _d

def reference(L0_attn_x, L0_attn_ln_g, L0_attn_ln_b, L0_attn_wq, L0_attn_bq, L0_attn_wk, L0_attn_bk, L0_attn_wv, L0_attn_bv, L0_attn_w0, L0_attn_b0, L0_ffn_router_w, L0_ffn_lora_down, L0_ffn_lora_up):

    def _L0_attn_ref(x, ln_g, ln_b, wq, bq, wk, bk, wv, bv, w0, b0):
        import jax, jax.numpy as jnp
        import numpy as np
        H = 16
        D = 64
        E = 128
        NEG_INF = float('-inf')

        def _layer_norm(x, g, b, eps=1e-05):
            mu = jnp.mean(x, axis=-1, keepdims=True)
            var = jnp.mean(jnp.square(x - mu), axis=-1, keepdims=True)
            return (x - mu) * jax.lax.rsqrt(var + eps) * g + b
        B, S, _ = x.shape
        residual = x
        xn = _layer_norm(x, ln_g, ln_b)
        q = (xn @ wq + bq).reshape(B, S, H, D).transpose(0, 2, 1, 3)
        k = (xn @ wk + bk).reshape(B, S, H, D).transpose(0, 2, 1, 3)
        v = (xn @ wv + bv).reshape(B, S, H, D).transpose(0, 2, 1, 3)
        scores = jnp.einsum('bhqd,bhkd->bhqk', q, k) / jnp.sqrt(jnp.float32(D))
        mask = jnp.tril(jnp.ones((S, S), bool), k=-1)
        scores = jnp.where(mask, NEG_INF, scores)
        a = jax.nn.softmax(scores, axis=-1)
        h = jnp.einsum('bhqk,bhkd->bhqd', a, v)
        h = h.transpose(0, 2, 1, 3).reshape(B, S, H * D)
        return h @ w0 + b0 + residual

    def _L0_ffn_ref(x, router_w, lora_down, lora_up):
        import jax, jax.numpy as jnp
        import numpy as np
        B, L, H = (32, 64, 128)
        E, R, TOP_K = (8, 16, 2)

        def _gates(cls, router_w):
            logits = jnp.einsum('bh,eh->be', cls, router_w)
            top_vals, top_idx = jax.lax.top_k(logits, TOP_K)
            mask = jnp.full_like(logits, -jnp.inf)
            rows = jnp.arange(logits.shape[0])[:, None]
            mask = mask.at[rows, top_idx].set(top_vals)
            return jax.nn.softmax(mask, axis=1)
        gates = _gates(x[:, 0, :], router_w)
        down = jnp.einsum('blh,erh->bler', x, lora_down)
        weighted = jnp.einsum('bler,ehr,be->blh', down, lora_up, gates)
        return x + weighted
    x = L0_attn_x
    x = x + _layernorm(_L0_attn_ref(_layernorm(x, axis=-1), L0_attn_ln_g, L0_attn_ln_b, L0_attn_wq, L0_attn_bq, L0_attn_wk, L0_attn_bk, L0_attn_wv, L0_attn_bv, L0_attn_w0, L0_attn_b0), axis=-1)
    x = x + _layernorm(_L0_ffn_ref(_layernorm(x, axis=-1), L0_ffn_router_w, L0_ffn_lora_down, L0_ffn_lora_up), axis=-1)
    return x

_drawn_inputs = setup_inputs


def setup_inputs(seed=0):
    import zlib

    import numpy as np

    out = dict(_drawn_inputs(seed))
    spreads = {'L0_attn_ln_g': (1.0, 0.6),
     'L0_attn_ln_b': (0.0, 0.325),
     'L0_attn_bq': (0.0, 0.8),
     'L0_attn_bk': (0.0, 2.0),
     'L0_attn_bv': (0.0, 0.28),
     'L0_attn_b0': (0.0, 0.1)}
    factors = {'L0_attn_wq': 7.414, 'L0_attn_wk': 7.365}
    for name, (base, spread) in spreads.items():
        noise = np.random.default_rng([zlib.crc32(name.encode()), seed]).standard_normal(out[name].shape)
        drawn = base * np.exp(spread * noise) if base else spread * noise
        out[name] = jnp.asarray(drawn.astype(out[name].dtype))
    for name, factor in factors.items():
        out[name] = (out[name] * factor).astype(out[name].dtype)
    return out
```

```python
import concourse.bass as bass
from concourse import mybir
from contextlib import ExitStack


def sandwich_kernel(nc, x, ln_gb, w_pairs, qk_bias, bv, w0, b0, router_t, down_t, up_r, out, xnt_dram, sums_dram):
    fp32, fp32r, bf16 = mybir.dt.float32, mybir.dt.float32r, mybir.dt.bfloat16
    ALU = mybir.AluOpType
    ACT = mybir.ActivationFunctionType
    AX = mybir.AxisListType
    P = 128
    T, E = x.shape
    B = 4
    S = T // B
    QB = S // P
    HD = w0.shape[0]
    D = 64
    PAIRS = HD // P
    N = B * PAIRS
    STEPS = 2 * QB
    HALF = S // 2
    HB = QB // 2
    EXPERTS = router_t.shape[1]
    RANK = P // EXPERTS
    EPS = 1e-5
    SCALE = D ** -0.5
    MASKED = -1e30

    TURNS = [[(c, min(4, QB - k // 2 - c)) for c in range(0, QB - k // 2, 4)] for k in range(STEPS)]
    TURN0 = [sum(len(t) for t in TURNS[:k]) for k in range(STEPS)]
    NTURN = sum(len(t) for t in TURNS)
    EVACS = NTURN // 2
    EVACS0 = TURN0[STEPS // 2] // 2
    W_DMAS, STACK_DMAS = 5, 6

    ctx = ExitStack()
    with ctx:
        def sb(name, shape, dt=fp32):
            return ctx.enter_context(nc.sbuf_tensor(name, shape, dt))

        def ps(name, shape, dt=fp32):
            return ctx.enter_context(nc.psum_tensor(name, shape, dt))

        def sem(name):
            return ctx.enter_context(nc.semaphore(name))

        ident = sb("ident", [P, P])
        ident_bf = sb("ident_bf", [P, P], bf16)
        mask_bf = sb("mask_bf", [P, P], bf16)
        ln_col = sb("ln_col", [P, 2])
        b0_row = sb("b0_row", [P, E])
        router_sb = sb("router_sb", [P, EXPERTS])
        down_sb = sb("down_sb", [P, P])
        up_sb = sb("up_sb", [P, E])
        minus_half = sb("minus_half", [P, QB])
        earlier = sb("earlier", [P, EXPERTS, EXPERTS])
        own = sb("own", [P, EXPERTS])
        wt = sb("wt", [P, 3, P])
        bias_col = sb("bias_col", [P, 2])
        bv_row = sb("bv_row", [P, P])
        w0_sb = sb("w0_sb", [P, E])
        xnt = sb("xnt", [P, S])
        q_raw = sb("q_raw", [P, S])
        k_raw = sb("k_raw", [P, S])
        q_low = sb("q_low", [P, S], fp32r)
        stacks = [sb(f"stacks{i}", [P, 6, S], fp32r) for i in range(2)]
        QA, QBS, KHA, KHB, KLA, KLB = range(6)
        v_sb = [sb(f"v_sb{i}", [P, QB, P]) for i in range(2)]
        probs = [sb(f"probs{i}", [P, S]) for i in range(2)]
        turned = sb("turned", [P, 2 * QB * HALF + 2 * HB * HALF])
        turned0 = turned[:, 0:2 * QB * HALF].rearrange("p (h j q) -> p h j q", h=2, j=QB)
        turned1 = turned[:, 2 * QB * HALF:].rearrange("p (h j q) -> p h j q", h=2, j=HB)
        neg_max = sb("neg_max", [P, STEPS])
        sums = [sb(f"sums{i}", [P, 2, QB]) for i in range(2)]
        inv_sums = sb("inv_sums", [P, 2, QB])
        inv_row = sb("inv_row", [P, S])
        o_raw = sb("o_raw", [P, S])
        o_norm = sb("o_norm", [P, S])
        acc = sb("acc", [P, T // P, E])
        stats = sb("stats", [P, QB, 6])
        moments = sb("moments", [P, 7, QB])
        gate = sb("gate", [P, 8, EXPERTS])
        rank8 = sb("rank8", [P, 2, EXPERTS, EXPERTS])
        first_tok = sb("first_tok", [P, P])

        def view(a, n, **kw):
            return turned[:, a:a + n].rearrange("p (t e) -> p t e", e=E)
        x_sb = view(0, T)
        xnt_all = turned[:, T:2 * T]
        ln_out = [view(2 * T + c * S, S) for c in range(2)]
        u_t = turned[:, 2 * T + 2 * S:2 * T + 3 * S]
        dg_t = turned[:, 2 * T + 3 * S:2 * T + 4 * S]

        sc = [ps(f"sc{i}", [P, S]) for i in range(2)]
        tp = [ps(f"tp{i}", [P, 512]) for i in range(2)]
        po = ps("po", [P, HALF])
        pp = ps("pp", [P, 512])

        s_x, s_small, s_const, s_b0 = sem("s_x"), sem("s_small"), sem("s_const"), sem("s_b0")
        s_dve, s_pow, s_var = sem("s_dve"), sem("s_pow"), sem("s_var")
        s_z, s_zt, s_xnt, s_xnt_out = sem("s_z"), sem("s_zt"), sem("s_xnt"), sem("s_xnt_out")
        s_xagain, s_u, s_ut, s_ut_out = sem("s_xagain"), sem("s_u"), sem("s_ut"), sem("s_ut_out")
        s_first, s_logit, s_lm, s_ge, s_gate = sem("s_first"), sem("s_logit"), sem("s_lm"), sem("s_ge"), sem("s_gate")
        s_down, s_dg, s_up, s_f, s_res, s_out = sem("s_down"), sem("s_dg"), sem("s_up"), sem("s_f"), sem("s_res"), sem("s_out")
        s_w = sem("s_w")
        s_w0 = sem("s_w0")
        s_qk = sem("s_qk")
        s_q_out = sem("s_q_out")
        s_k_out = sem("s_k_out")
        s_q_high = sem("s_q_high")
        s_k_high = sem("s_k_high")
        s_cut = sem("s_cut")
        s_q_cut = sem("s_q_cut")
        s_k_cut = sem("s_k_cut")
        s_stack = sem("s_stack")
        s_v = sem("s_v")
        s_v_out = sem("s_v_out")
        s_score = sem("s_score")
        s_max = sem("s_max")
        s_exp = sem("s_exp")
        s_turn = sem("s_turn")
        s_ta, s_td = sem("s_ta"), sem("s_td")
        s_pv0, s_pv1 = sem("s_pv0"), sem("s_pv1")
        s_o_out = sem("s_o_out")
        s_inv = sem("s_inv")
        s_inv_out = sem("s_inv_out")
        s_inv_row = sem("s_inv_row")
        s_norm = sem("s_norm")
        s_w0p = sem("s_w0p")
        s_acc = sem("s_acc")

        block = ctx.enter_context(nc.Block())

        def pairs(eng, body):
            body(0, 0, True, False)
            body(1, 1, False, False)
            with eng.Fori(0, (N - 4) // 2) as t:
                body(t * 2 + 2, 0, False, False)
                body(t * 2 + 3, 1, False, False)
            body(N - 2, 0, False, False)
            body(N - 1, 1, False, True)

        def reach(eng, semaphore, count):
            if not (isinstance(count, int) and count == 0):
                eng.wait_ge(semaphore, count)

        @block.sync
        def _(sp):
            xt = x.rearrange("(t p) e -> p t e", p=P)
            for c in range(B):
                sp.dma_start(x_sb[:, c * QB:(c + 1) * QB, :], xt[:, c * QB:(c + 1) * QB, :]).then_inc(s_x, 16)
            for dst, src in ((ln_col[:], ln_gb), (router_sb[:], router_t), (down_sb[:], down_t),
                             (up_sb[:], up_r), (b0_row[:], b0.to_broadcast([P, E]))):
                sp.dma_start(dst, src).then_inc(s_small, 16)

            def load_weights(n):
                p, b, column = n % PAIRS, (n // PAIRS) * S, (n % PAIRS) * P
                sp.dma_start(wt[:].rearrange("p a c -> p (a c)"),
                             w_pairs[bass.ds(p, 1), :, :].rearrange("o p n -> (o p) n")).then_inc(s_w, 16)
                sp.dma_start(bias_col[:], qk_bias[bass.ds(p, 1), :, :].rearrange("o p n -> (o p) n")).then_inc(s_w, 16)
                sp.dma_start(bv_row[:], bv[0:1, bass.ds(column, P)].to_broadcast([P, P])).then_inc(s_w, 16)
                for c in range(2):
                    sp.dma_start(xnt[:, c * HALF:(c + 1) * HALF],
                                 xnt_dram[:, bass.ds(b + c * HALF, HALF)]).then_inc(s_w, 16)

            def build_stacks(n, parity):
                st, q_lo = stacks[parity][:].bitcast(fp32), q_low[:].bitcast(fp32)
                sp.wait_ge(s_q_cut, n + 1)
                sp.dma_start(st[D:P, QA, :], q_lo[0:D, :]).then_inc(s_stack, 16)
                sp.dma_start(st[0:D, QBS, :], q_lo[D:P, :]).then_inc(s_stack, 16)
                sp.wait_ge(s_k_cut, n + 1)
                for k in (KHA, KLA):
                    sp.dma_start(st[D:P, k, :], st[0:D, k, :]).then_inc(s_stack, 16)
                for k in (KHB, KLB):
                    sp.dma_start(st[0:D, k, :], st[D:P, k, :]).then_inc(s_stack, 16)

            for c in range(B):
                sp.wait_ge(s_xnt, 2 * (c + 1))
                sp.dma_start(xnt_dram[:, c * S:(c + 1) * S], xnt_all[:, c * S:(c + 1) * S]).then_inc(s_xnt_out, 16)
            sp.wait_ge(s_xnt_out, 16 * B)
            load_weights(0)
            build_stacks(0, 0)
            sp.wait_ge(s_v_out, 2)
            sp.wait_ge(s_k_out, 2)
            load_weights(1)

            def spread_sums(g):
                sp.wait_ge(s_inv, g + 1)
                sp.dma_start(sums_dram.rearrange("h p i -> p h i"), inv_sums[:]).then_inc(s_inv_out, 16)
                sp.wait_ge(s_inv_out, 16 * (g + 1))
                for h in range(2):
                    sp.dma_start(inv_row[h * D:(h + 1) * D, :],
                                 sums_dram[h:h + 1, :, :].rearrange("o p i -> o (p i)").to_broadcast([D, S])
                                 ).then_inc(s_inv_row, 16)

            def pair(g, parity, first, last):
                if not first:
                    spread_sums(g - 1)
                if not last:
                    build_stacks(g + 1, 1 - parity)
                if not last:
                    sp.wait_ge(s_v_out, 2 * g + 4)
                    sp.wait_ge(s_k_out, 2 * g + 4)
                    load_weights((g + 2) % N)
                if not first:
                    sp.wait_ge(s_acc, 2 * g)
                sp.dma_start(w0_sb[:], w0[bass.ds((g % PAIRS) * P, P), :]).then_inc(s_w0, 16)

            pairs(sp, pair)
            spread_sums(N - 1)
            sp.wait_ge(s_pv0, N)
            sp.wait_ge(s_pv1, N)
            for c in range(B):
                sp.dma_start(x_sb[:, c * QB:(c + 1) * QB, :], xt[:, c * QB:(c + 1) * QB, :]).then_inc(s_xagain, 16)
            ot = out.rearrange("(t p) e -> p t e", p=P)
            for c in range(B):
                sp.wait_ge(s_res, c + 1)
                sp.dma_start(ot[:, c * QB:(c + 1) * QB, :], acc[:, c * QB:(c + 1) * QB, :]).then_inc(s_out, 16)
            sp.wait_ge(s_out, 16 * B)
            sp.wait_ge(s_w, 16 * W_DMAS * (N + 1))

        @block.gpsimd
        def _(pool):
            nc.gpsimd.memset(minus_half[:], -0.5)
            nc.gpsimd.memset(ident[:], 0.0)
            nc.gpsimd.memset(ident_bf[:], 0.0)
            nc.gpsimd.memset(mask_bf[:], 0.0)
            nc.gpsimd.memset(earlier[:], 1.0)
            nc.gpsimd.memset(own[:], 1.0).then_inc(s_const, 1)
            pool.wait_ge(s_const, 1)
            nc.gpsimd.affine_select(out=ident[:], in_=ident[:], compare_op=ALU.not_equal, fill=1.0, base=0,
                                    pattern=[[-1, P]], channel_multiplier=1)
            nc.gpsimd.affine_select(out=ident_bf[:], in_=ident_bf[:], compare_op=ALU.not_equal, fill=1.0, base=0,
                                    pattern=[[-1, P]], channel_multiplier=1)
            nc.gpsimd.affine_select(out=mask_bf[:], in_=mask_bf[:], compare_op=ALU.is_ge, fill=MASKED, base=0,
                                    pattern=[[1, P]], channel_multiplier=-1)
            nc.gpsimd.affine_select(out=earlier[:], in_=earlier[:], compare_op=ALU.is_ge, fill=0.0, base=-1,
                                    pattern=[[1, EXPERTS], [-1, EXPERTS]], channel_multiplier=0)
            nc.gpsimd.affine_select(out=own[:], in_=own[:], compare_op=ALU.is_ge, fill=0.0, base=0,
                                    pattern=[[-RANK, EXPERTS]], channel_multiplier=1).then_inc(s_const, 1)
            pool.wait_ge(s_const, 2)
            nc.gpsimd.affine_select(out=own[:], in_=own[:], compare_op=ALU.is_ge, fill=0.0, base=RANK - 1,
                                    pattern=[[RANK, EXPERTS]], channel_multiplier=-1).then_inc(s_const, 1)

            def inverse_roots(first, count):
                for n in range(first, first + count):
                    pool.wait_ge(s_var, n + 1)
                    nc.gpsimd.tensor_tensor(moments[:, 6, :], moments[:, 5, :], minus_half[:], ALU.pow).then_inc(s_pow, 1)

            inverse_roots(0, 2 * B)

            def low(dst, src, hi):
                return nc.gpsimd.tensor_tensor(dst, src, hi.bitcast(fp32), ALU.subtract)

            def cut_q(n, parity, first):
                st = stacks[parity]
                pool.wait_ge(s_q_high, n + 1)
                if not first:
                    pool.wait_ge(s_k_cut, n)
                    pool.wait_ge(s_stack, 16 * STACK_DMAS * n)
                low(q_low[0:D, :], q_raw[0:D, :], st[0:D, QA, :]).then_inc(s_cut, 1)
                pool.wait_ge(s_cut, 2 * n + 1)
                low(q_low[D:P, :], q_raw[D:P, :], st[D:P, QBS, :]).then_inc(s_q_cut, 1)

            def cut_k(n, parity):
                st = stacks[parity]
                if isinstance(n, int) and n <= 1:
                    pool.wait_ge(s_q_cut, n + 1)
                else:
                    reach(pool, s_norm, 2 * (n - 1))
                pool.wait_ge(s_k_high, n + 1)
                low(st[0:D, KLA, :], k_raw[0:D, :], st[0:D, KHA, :]).then_inc(s_cut, 1)
                pool.wait_ge(s_cut, 2 * n + 2)
                low(st[D:P, KLB, :], k_raw[D:P, :], st[D:P, KHB, :]).then_inc(s_k_cut, 1)

            def normalise(g, before, count):
                inv = inv_row[:].rearrange("p (q i) -> p i q", i=QB)
                pool.wait_ge(before, count)
                pool.wait_ge(s_inv_row, 32 * (g + 1))
                reach(pool, s_w0p, 2 * g)
                for half in range(2):
                    pool.wait_ge(s_o_out, 2 * g + 1 + half)
                    if half:
                        pool.wait_ge(s_norm, 2 * g + 1)
                    q = slice(half * HALF, (half + 1) * HALF)
                    nc.gpsimd.tensor_tensor(o_norm[:, q].rearrange("p (i q) -> p i q", q=P),
                                            o_raw[:, q].rearrange("p (i q) -> p i q", q=P),
                                            inv[:, half * HB:(half + 1) * HB, :], ALU.mult).then_inc(s_norm, 1)

            pool.wait_ge(s_pow, 2 * B)
            cut_q(0, 0, True)
            cut_k(0, 0)

            def pair(g, parity, first, last):
                if not last:
                    cut_q(g + 1, 1 - parity, False)
                if not first:
                    normalise(g - 1, *((s_k_cut, N) if last else (s_q_cut, g + 2)))
                if not last:
                    cut_k(g + 1, 1 - parity)

            pairs(pool, pair)
            normalise(N - 1, s_norm, 2 * (N - 1))
            inverse_roots(2 * B, 3 * B)

        @block.tensor
        def _(pe):
            pe.wait_ge(s_const, 3)
            for c in range(B):
                for a in range(2):
                    pe.wait_ge(s_z, c + 1)
                    if c:
                        pe.wait_ge(s_xnt, 2 * (c - 1) + a + 1)
                    for j in range(4):
                        last = nc.tensor.transpose(tp[a][:, j * P:(j + 1) * P], ln_out[c % 2][:, 4 * a + j, :], ident[:])
                    last.then_inc(s_zt, 1)

            def project(n, part):
                if part == 0:
                    pe.wait_ge(s_w, 16 * W_DMAS * (n + 1))
                c = part % 2
                nc.tensor.matmul(pp[:], wt[:, part // 2, :], xnt[:, c * HALF:(c + 1) * HALF],
                                 start=True, stop=True).then_inc(s_qk, 1)

            def project_v(n, c):
                for j in range(4):
                    t = 4 * c + j
                    last = nc.tensor.matmul(pp[:, j * P:(j + 1) * P], xnt[:, t * P:(t + 1) * P], wt[:, 2, :],
                                            start=True, stop=True)
                last.then_inc(s_v, 1)

            def scores(g, parity, k):
                i, h = k // 2, k % 2
                st = stacks[parity]
                width = (QB - i) * P
                for o in range(0, width, 512):
                    w = min(512, width - o)
                    dst = sc[k % 2][:, o:o + w]
                    q = st[:, QA + h, i * P:(i + 1) * P]
                    keys = slice(i * P + o, i * P + o + w)
                    nc.tensor.matmul(dst, q, st[:, KHA + h, keys], start=True, stop=False)
                    last = nc.tensor.matmul(dst, q, st[:, KLA + h, keys], start=False, stop=(o > 0))
                    if o == 0:
                        last = nc.tensor.matmul(dst[:, 0:P], ident_bf[:], mask_bf[:], start=False, stop=True)
                last.then_inc(s_score, 1)

            def turn(g, k):
                pe.wait_ge(s_exp, STEPS * g + k + 1)
                for n, (c0, m) in enumerate(TURNS[k]):
                    t = TURN0[k] + n
                    if t >= 2 or not (isinstance(g, int) and g == 0):
                        pe.wait_ge((s_ta, s_td)[t % 2], EVACS * g + t // 2)
                    for j in range(m):
                        last = nc.tensor.transpose(tp[t % 2][:, j * P:(j + 1) * P],
                                                   probs[k % 2][:, (c0 + j) * P:(c0 + j + 1) * P], ident[:])
                    last.then_inc(s_turn, 1)

            def outputs(g, parity, half, blocks):
                for j in blocks:
                    w = min(HB, j + 1 - half * HB) * P
                    for h in range(2):
                        src = (turned0 if half == 0 else turned1)[:, h, j - half * HB, 0:w]
                        last = nc.tensor.matmul(po[h * D:(h + 1) * D, 0:w], v_sb[parity][:, j, h * D:(h + 1) * D],
                                                src, start=(j == QB - 1), stop=(j == half * HB))
                if j == half * HB:
                    last.then_inc((s_pv0, s_pv1)[half], 1)

            def project_out(g, c):
                pe.wait_ge(s_norm, 2 * g + 1 + c)
                if c == 0:
                    pe.wait_ge(s_w0, 16 * (g + 1))
                for j in range(4):
                    t = 4 * c + j
                    last = nc.tensor.matmul(pp[:, j * P:(j + 1) * P], o_norm[:, t * P:(t + 1) * P], w0_sb[:],
                                            start=True, stop=True)
                last.then_inc(s_w0p, 1)

            project(0, 0)
            pe.wait_ge(s_q_out, 1)
            project(0, 1)
            pe.wait_ge(s_q_out, 2)
            project(0, 2)
            pe.wait_ge(s_k_out, 1)
            project(0, 3)
            pe.wait_ge(s_k_out, 2)
            project_v(0, 0)
            pe.wait_ge(s_v_out, 1)
            project_v(0, 1)

            def pair(g, parity, first, last):
                n = g + 1
                for k in range(STEPS):
                    if k == 0:
                        pe.wait_ge(s_stack, 16 * STACK_DMAS * (g + 1))
                    if k > 1 or not first:
                        pe.wait_ge(s_exp, STEPS * g + k - 1)
                    scores(g, parity, k)
                    if k == 0 and not last:
                        pe.wait_ge(s_v_out, 2 * g + 2)
                        if not first:
                            reach(pe, s_acc, 2 * (g - 1))
                        project(n, 0)
                    if k == 1 and not last:
                        pe.wait_ge(s_q_out, 2 * n + 1)
                        project(n, 1)
                    if k == 2 and not first:
                        pe.wait_ge(s_ta, EVACS * g)
                        pe.wait_ge(s_td, EVACS * g)
                        pe.wait_ge(s_o_out, 2 * g - 1)
                        outputs(g - 1, 1 - parity, 1, (7, 6))
                    if k == 3 and not last:
                        pe.wait_ge(s_q_out, 2 * n + 2)
                        project(n, 2)
                    if k == 4 and not first:
                        outputs(g - 1, 1 - parity, 1, (5, 4))
                    if k == 5 and not last:
                        pe.wait_ge(s_k_out, 2 * n + 1)
                        project(n, 3)
                    if k == 6 and not last:
                        pe.wait_ge(s_k_out, 2 * n + 2)
                        project_v(n, 0)
                    if k == 7 and not last:
                        pe.wait_ge(s_v_out, 2 * n + 1)
                        project_v(n, 1)
                    if k == 8 and not first:
                        pe.wait_ge(s_v_out, 2 * (g + 1) if last else 2 * n + 2)
                        project_out(g - 1, 0)
                    if k == 9:
                        pe.wait_ge(s_ta, EVACS * g + EVACS0)
                        pe.wait_ge(s_td, EVACS * g + EVACS0)
                        if not first:
                            pe.wait_ge(s_o_out, 2 * g)
                        outputs(g, parity, 0, (7,))
                    if 10 <= k <= 13:
                        outputs(g, parity, 0, (16 - k,))
                    if k == 14:
                        outputs(g, parity, 0, (2, 1, 0))
                    if k == 15 and not first:
                        pe.wait_ge(s_acc, 2 * (g - 1) + 1)
                        project_out(g - 1, 1)
                    if k:
                        turn(g, k - 1)
                    elif not first:
                        turn(g - 1, STEPS - 1)

            pairs(pe, pair)
            g = N - 1
            turn(g, STEPS - 1)
            pe.wait_ge(s_ta, EVACS * N)
            pe.wait_ge(s_td, EVACS * N)
            pe.wait_ge(s_o_out, 2 * g + 1)
            outputs(g, 1, 1, (7, 6, 5, 4))
            pe.wait_ge(s_acc, 2 * g)
            project_out(g, 0)
            pe.wait_ge(s_acc, 2 * g + 1)
            project_out(g, 1)

            for c in range(B):
                pe.wait_ge(s_u, c + 1)
                for a in range(2):
                    if c:
                        pe.wait_ge(s_ut_out, 2 * (c - 1) + a + 1)
                    for j in range(4):
                        last = nc.tensor.transpose(tp[a][:, j * P:(j + 1) * P], ln_out[c % 2][:, 4 * a + j, :], ident[:])
                    last.then_inc(s_ut, 1)
                pe.wait_ge(s_first, c + 1)
                nc.tensor.matmul(pp[:, 0:EXPERTS], first_tok[:], router_sb[:], start=True, stop=True).then_inc(s_logit, 1)
                pe.wait_ge(s_ut_out, 2 * (c + 1))
                if c:
                    pe.wait_ge(s_dg, 2 * c)
                for a in range(2):
                    nc.tensor.matmul(sc[0][:, a * 512:(a + 1) * 512], down_sb[:], u_t[:, a * 512:(a + 1) * 512],
                                     start=True, stop=True).then_inc(s_down, 1)
                pe.wait_ge(s_dg, 2 * (c + 1))
                if c:
                    pe.wait_ge(s_f, c)
                for t in range(QB):
                    last = nc.tensor.matmul(sc[1][:, t * P:(t + 1) * P], dg_t[:, t * P:(t + 1) * P], up_sb[:],
                                            start=True, stop=True)
                last.then_inc(s_up, 1)

        @block.scalar
        def _(act):
            act.wait_ge(s_small, 16 * 5)
            for c in range(B):
                for a in range(2):
                    act.wait_ge(s_zt, 2 * c + a + 1)
                    nc.scalar.activation(xnt_all[:, c * S + a * 512:c * S + (a + 1) * 512], tp[a][:], ACT.Identity,
                                         bias=ln_col[:, 1:2], scale=ln_col[:, 0:1]).then_inc(s_xnt, 1)

            def take_k(n, c, wait):
                act.wait_ge(s_qk, 4 * n + 3 + c)
                if wait:
                    act.wait_ge(s_k_cut, n)
                nc.scalar.activation(k_raw[:, c * HALF:(c + 1) * HALF], pp[:], ACT.Identity,
                                     bias=bias_col[:, 1:2]).then_inc(s_k_out, 1)

            def take_o(g, half):
                act.wait_ge((s_pv0, s_pv1)[half], g + 1)
                if not (isinstance(g, int) and g == 0):
                    act.wait_ge(s_norm, 2 * (g - 1) + 1 + half)
                nc.scalar.copy(o_raw[:, half * HALF:(half + 1) * HALF], po[:]).then_inc(s_o_out, 1)

            def take_turn(g, k):
                i, h = k // 2, k % 2
                for n, (c0, m) in enumerate(TURNS[k]):
                    t = TURN0[k] + n
                    if t % 2:
                        continue
                    reach(act, s_pv0 if i < HB else s_pv1, g)
                    act.wait_ge(s_turn, NTURN * g + t + 1)
                    dst, at = (turned0, 0) if i < HB else (turned1, HB)
                    nc.scalar.copy(dst[:, h, i + c0 - at:i + c0 - at + m, (i - at) * P:(i - at + 1) * P],
                                   tp[0][:, 0:m * P].rearrange("p (j q) -> p j q", q=P)).then_inc(s_ta, 1)

            act.wait_ge(s_w, 16 * W_DMAS)
            take_k(0, 0, False)
            take_k(0, 1, False)
            act.wait_ge(s_xnt_out, 16 * B)

            def pair(g, parity, first, last):
                for k in range(STEPS):
                    i, h = k // 2, k % 2
                    width = (QB - i) * P
                    act.wait_ge(s_max, STEPS * g + k + 1)
                    if k == 0 and not first:
                        act.wait_ge(s_inv, g)
                    nc.scalar.activation(probs[k % 2][:, 0:width], sc[k % 2][:, 0:width], ACT.Exp,
                                         bias=neg_max[:, k:k + 1],
                                         accum_out=sums[parity][:, h, i:i + 1]).then_inc(s_exp, 1)
                    if k == 3 and not last:
                        take_k(g + 1, 0, True)
                    if k == 4 and not first:
                        take_o(g - 1, 1)
                    if k == 5 and not last:
                        take_k(g + 1, 1, True)
                    if k == 14:
                        take_o(g, 0)
                    if k:
                        take_turn(g, k - 1)
                    elif not first:
                        take_turn(g - 1, STEPS - 1)

            pairs(act, pair)
            take_turn(N - 1, STEPS - 1)
            take_o(N - 1, 1)

            for c in range(B):
                for a in range(2):
                    act.wait_ge(s_ut, 2 * c + a + 1)
                    if c and a == 0:
                        act.wait_ge(s_down, 2 * c)
                    nc.scalar.copy(u_t[:, a * 512:(a + 1) * 512], tp[a][:]).then_inc(s_ut_out, 1)
                    if a == 0:
                        act.wait_ge(s_ut_out, 2 * c + 1)
                        if c:
                            act.wait_ge(s_logit, c)
                        nc.scalar.copy(first_tok[:], u_t[:, 0:1].to_broadcast([P, P])).then_inc(s_first, 1)
                act.wait_ge(s_lm, c + 1)
                nc.scalar.activation(gate[:, 2, :], gate[:, 0, :], ACT.Exp, bias=gate[:, 1, 0:1]).then_inc(s_ge, 1)
                act.wait_ge(s_gate, c + 1)
                for a in range(2):
                    act.wait_ge(s_down, 2 * c + a + 1)
                    if c:
                        act.wait_ge(s_up, c)
                    nc.scalar.activation(dg_t[:, a * 512:(a + 1) * 512], sc[0][:, a * 512:(a + 1) * 512], ACT.Copy,
                                         scale=gate[:, 7, 0:1]).then_inc(s_dg, 1)

        @block.vector
        def _(dve):
            chain = [0]
            var = [0]

            def link(ins):
                chain[0] += 1
                ins.then_inc(s_dve, 1)
                dve.wait_ge(s_dve, chain[0])

            def layernorm(dst, src):
                for t in range(QB):
                    last = nc.vector.bn_stats(stats[:, t, :], src[:, t, :])
                link(last)
                me, qe, mo, qo = (stats[:, :, a:a + 1].rearrange("p t o -> p (t o)") for a in (1, 2, 4, 5))
                nc.vector.tensor_tensor(moments[:, 0, :], me, mo, ALU.add)
                nc.vector.tensor_tensor(moments[:, 1, :], me, mo, ALU.subtract)
                link(nc.vector.tensor_tensor(moments[:, 2, :], qe, qo, ALU.add))
                nc.vector.tensor_scalar(moments[:, 3, :], moments[:, 0, :], 0.5, None, ALU.mult)
                link(nc.vector.tensor_tensor(moments[:, 4, :], moments[:, 1, :], moments[:, 1, :], ALU.mult))
                link(nc.vector.scalar_tensor_tensor(out=moments[:, 4, :], in0=moments[:, 4, :], scalar=E / 4,
                                                    in1=moments[:, 2, :], op0=ALU.mult, op1=ALU.add))
                nc.vector.tensor_scalar(moments[:, 5, :], moments[:, 4, :], 1.0 / E, EPS, ALU.mult,
                                        ALU.add).then_inc(s_var, 1)
                link(nc.vector.tensor_tensor(dst, src, moments[:, 3, :].unsqueeze(2).to_broadcast([P, QB, E]),
                                             ALU.subtract))
                var[0] += 1
                dve.wait_ge(s_pow, var[0])
                return nc.vector.tensor_tensor(dst, dst, moments[:, 6, :].unsqueeze(2).to_broadcast([P, QB, E]),
                                               ALU.mult)

            dve.wait_ge(s_small, 16 * 5)
            dve.wait_ge(s_x, 16 * B)
            for c in range(B):
                y = acc[:, c * QB:(c + 1) * QB, :]
                link(layernorm(y, x_sb[:, c * QB:(c + 1) * QB, :]))
                if c >= 2:
                    dve.wait_ge(s_zt, 2 * (c - 1))
                link(layernorm(ln_out[c % 2], y))
                nc.vector.tensor_tensor(y, y, b0_row[:].unsqueeze(1).to_broadcast([P, QB, E]), ALU.add
                                        ).then_inc(s_z, 1)

            def take_q(n, c, wait):
                dve.wait_ge(s_qk, 4 * n + 1 + c)
                if wait:
                    dve.wait_ge(s_q_cut, n)
                nc.vector.tensor_scalar(q_raw[:, c * HALF:(c + 1) * HALF], pp[:], bias_col[:, 0:1], SCALE,
                                        ALU.add, ALU.mult).then_inc(s_q_out, 1)

            def high_q(n, parity):
                dve.wait_ge(s_q_out, 2 * n + 2)
                nc.vector.tensor_copy(stacks[parity][0:D, QA, :], q_raw[0:D, :])
                nc.vector.tensor_copy(stacks[parity][D:P, QBS, :], q_raw[D:P, :]).then_inc(s_q_high, 1)

            def high_k(n, parity):
                dve.wait_ge(s_k_out, 2 * n + 2)
                nc.vector.tensor_copy(stacks[parity][0:D, KHA, :], k_raw[0:D, :])
                nc.vector.tensor_copy(stacks[parity][D:P, KHB, :], k_raw[D:P, :]).then_inc(s_k_high, 1)

            def take_v(n, parity, c, wait):
                dve.wait_ge(s_v, 2 * n + 1 + c)
                if wait:
                    reach(dve, s_pv1, n - 1)
                nc.vector.tensor_tensor(v_sb[parity][:, 4 * c:4 * c + 4, :],
                                        pp[:].rearrange("p (j d) -> p j d", d=P),
                                        bv_row[:].unsqueeze(1).to_broadcast([P, 4, P]), ALU.add).then_inc(s_v_out, 1)

            def take_turn(g, k):
                i, h = k // 2, k % 2
                for n, (c0, m) in enumerate(TURNS[k]):
                    t = TURN0[k] + n
                    if t % 2 == 0:
                        continue
                    reach(dve, s_pv0 if i < HB else s_pv1, g)
                    dve.wait_ge(s_turn, NTURN * g + t + 1)
                    dst, at = (turned0, 0) if i < HB else (turned1, HB)
                    nc.vector.tensor_copy(dst[:, h, i + c0 - at:i + c0 - at + m, (i - at) * P:(i - at + 1) * P],
                                          tp[1][:, 0:m * P].rearrange("p (j q) -> p j q", q=P)).then_inc(s_td, 1)

            def invert_sums(g, parity):
                dve.wait_ge(s_exp, STEPS * (g + 1))
                reach(dve, s_inv_out, 16 * g)
                reach(dve, s_norm, 2 * g)
                nc.vector.reciprocal(inv_sums[:], sums[parity][:]).then_inc(s_inv, 1)

            def add_out(g, c):
                dve.wait_ge(s_w0p, 2 * g + 1 + c)
                reach(dve, s_acc, 2 * g)
                a = acc[:].rearrange("p t e -> p (t e)")[:, bass.ds((g // PAIRS) * (QB * E) + c * 512, 512)]
                nc.vector.tensor_tensor(a, pp[:], a, ALU.add).then_inc(s_acc, 1)

            dve.wait_ge(s_w, 16 * W_DMAS)
            take_q(0, 0, False)
            take_q(0, 1, False)
            high_q(0, 0)
            high_k(0, 0)
            take_v(0, 0, 0, False)
            take_v(0, 0, 1, False)
            dve.wait_ge(s_xnt_out, 16 * B)

            def pair(g, parity, first, last):
                for k in range(STEPS):
                    i, h = k // 2, k % 2
                    width = (QB - i) * P
                    dve.wait_ge(s_score, STEPS * g + k + 1)
                    nc.vector.tensor_reduce(neg_max[:, k:k + 1], sc[k % 2][:, 0:width], AX.X, ALU.max,
                                            negate=True).then_inc(s_max, 1)
                    if k == 0 and not first:
                        invert_sums(g - 1, 1 - parity)
                    if k < 2 and not last:
                        take_q(g + 1, k, True)
                    if k == 2 and not last:
                        high_q(g + 1, 1 - parity)
                    if k == 6 and not last:
                        high_k(g + 1, 1 - parity)
                    if k in (6, 7) and not last:
                        take_v(g + 1, 1 - parity, k - 6, not first)
                    if k == 8 and not first:
                        add_out(g - 1, 0)
                    if k == 15 and not first:
                        add_out(g - 1, 1)
                    if k:
                        take_turn(g, k - 1)
                    elif not first:
                        take_turn(g - 1, STEPS - 1)

            pairs(dve, pair)
            take_turn(N - 1, STEPS - 1)
            invert_sums(N - 1, 1)
            add_out(N - 1, 0)
            add_out(N - 1, 1)
            dve.wait_ge(s_acc, 2 * N)
            dve.wait_ge(s_xagain, 16 * B)
            for c in range(B):
                x1 = x_sb[:, c * QB:(c + 1) * QB, :]
                res = acc[:, c * QB:(c + 1) * QB, :]
                u = ln_out[c % 2]
                link(layernorm(res, res))
                link(nc.vector.tensor_tensor(x1, x1, res, ALU.add))
                layernorm(u, x1).then_inc(s_u, 1)
                dve.wait_ge(s_logit, c + 1)
                link(nc.vector.tensor_copy(gate[:, 0, :], pp[:, 0:EXPERTS]))
                link(nc.vector.tensor_reduce(gate[:, 1, 0:1], gate[:, 0, :], AX.X, ALU.max, negate=True))
                mine = gate[:, 0, :].unsqueeze(2).to_broadcast([P, EXPERTS, EXPERTS])
                others = gate[:, 0, :].unsqueeze(1).to_broadcast([P, EXPERTS, EXPERTS])
                nc.vector.tensor_tensor(rank8[:, 0], others, mine, ALU.is_equal).then_inc(s_lm, 1)
                link(nc.vector.tensor_tensor(rank8[:, 1], others, mine, ALU.is_gt))
                link(nc.vector.tensor_tensor(rank8[:, 0], rank8[:, 0], earlier[:], ALU.mult))
                link(nc.vector.tensor_tensor(rank8[:, 0], rank8[:, 0], rank8[:, 1], ALU.add))
                link(nc.vector.tensor_reduce(gate[:, 3, :], rank8[:, 0], AX.X, ALU.add))
                link(nc.vector.tensor_scalar(gate[:, 3, :], gate[:, 3, :], 2.0, None, ALU.is_lt))
                dve.wait_ge(s_ge, c + 1)
                link(nc.vector.tensor_tensor(gate[:, 4, :], gate[:, 2, :], gate[:, 3, :], ALU.mult))
                nc.vector.tensor_tensor(gate[:, 5, :], gate[:, 4, :], own[:], ALU.mult)
                link(nc.vector.tensor_reduce(gate[:, 6, 0:1], gate[:, 4, :], AX.X, ALU.add))
                nc.vector.tensor_reduce(gate[:, 6, 1:2], gate[:, 5, :], AX.X, ALU.add)
                link(nc.vector.reciprocal(gate[:, 6, 2:3], gate[:, 6, 0:1]))
                if c:
                    dve.wait_ge(s_dg, 2 * c)
                nc.vector.tensor_tensor(gate[:, 7, 0:1], gate[:, 6, 1:2], gate[:, 6, 2:3],
                                        ALU.mult).then_inc(s_gate, 1)
                dve.wait_ge(s_up, c + 1)
                flat = u.rearrange("p t e -> p (t e)")
                nc.vector.tensor_tensor(flat, sc[1][:], flat, ALU.add).then_inc(s_f, 1)
                dve.wait_ge(s_f, c + 1)
                link(layernorm(res, u))
                nc.vector.tensor_tensor(res, res, x1, ALU.add).then_inc(s_res, 1)


def kernel(**inputs):
    import numpy as np
    import concourse.bacc as bacc
    from concourse import mybir as mb
    from concourse.bass_utils import run_bass_kernel_spmd as run

    def a(name):
        return np.asarray(inputs[name])

    x = a("L0_attn_x")
    pairs = a("L0_attn_wq").shape[1] // 128

    def by_pair(w):
        return w.reshape(w.shape[0], pairs, 128).transpose(1, 0, 2)

    down, up = a("L0_ffn_lora_down"), a("L0_ffn_lora_up")
    arrays = {
        "x": x.reshape(-1, x.shape[-1]),
        "ln_gb": np.stack([a("L0_attn_ln_g"), a("L0_attn_ln_b")], axis=1),
        "w_pairs": np.concatenate([by_pair(a(f"L0_attn_w{c}")) for c in "qkv"], axis=2),
        "qk_bias": np.stack([a("L0_attn_bq").reshape(pairs, 128), a("L0_attn_bk").reshape(pairs, 128)], axis=2),
        "bv": a("L0_attn_bv").reshape(1, -1),
        "w0": a("L0_attn_w0"),
        "b0": a("L0_attn_b0").reshape(1, -1),
        "router_t": a("L0_ffn_router_w").T,
        "down_t": down.reshape(-1, down.shape[-1]).T,
        "up_r": up.transpose(0, 2, 1).reshape(-1, up.shape[1]),
    }
    arrays = {n: np.ascontiguousarray(v) for n, v in arrays.items()}
    nc = bacc.Bacc("TRN2", target_bir_lowering=False, num_devices=1)
    f32 = mb.dt.float32
    args = {n: nc.dram_tensor(n, v.shape, mb.dt.from_np(v.dtype), kind="ExternalInput").ap() for n, v in arrays.items()}
    out = nc.dram_tensor("out", arrays["x"].shape, f32, kind="ExternalOutput").ap()
    xnt = nc.dram_tensor("xnt_dram", (128, arrays["x"].shape[0]), f32).ap()
    sums = nc.dram_tensor("sums_dram", (2, 128, 8), f32).ap()
    sandwich_kernel(nc, out=out, xnt_dram=xnt, sums_dram=sums, **args)
    r = run(nc, [arrays], core_ids=[0])
    return r.results[0]["out"].reshape(x.shape)
```

```python
import concourse.bass as bass
from concourse import mybir
from contextlib import ExitStack


def sandwich_kernel(nc, x, ln_gb, w_pairs, qk_bias, bv, w0, b0, router_t, down_t, up_r, out, xnt_dram, sums_dram):
    fp32, fp32r, bf16 = mybir.dt.float32, mybir.dt.float32r, mybir.dt.bfloat16
    ALU = mybir.AluOpType
    ACT = mybir.ActivationFunctionType
    AX = mybir.AxisListType
    P = 128
    T, E = x.shape
    B = 4
    S = T // B
    QB = S // P
    HD = w0.shape[0]
    D = 64
    PAIRS = HD // P
    N = B * PAIRS
    STEPS = 2 * QB
    HALF = S // 2
    HB = QB // 2
    EXPERTS = router_t.shape[1]
    RANK = P // EXPERTS
    EPS = 1e-5
    SCALE = D ** -0.5
    MASKED = -1e30

    TURNS = [[(c, min(4, QB - k // 2 - c)) for c in range(0, QB - k // 2, 4)] for k in range(STEPS)]
    TURN0 = [sum(len(t) for t in TURNS[:k]) for k in range(STEPS)]
    NTURN = sum(len(t) for t in TURNS)
    EVACS = NTURN // 2
    EVACS0 = TURN0[STEPS // 2] // 2
    W_DMAS, STACK_DMAS = 4, 6
    A_LINKS, B_LINKS = 9, 21

    ctx = ExitStack()
    with ctx:
        def sb(name, shape, dt=fp32):
            return ctx.enter_context(nc.sbuf_tensor(name, shape, dt))

        def ps(name, shape, dt=fp32):
            return ctx.enter_context(nc.psum_tensor(name, shape, dt))

        def sem(name):
            return ctx.enter_context(nc.semaphore(name))

        ident = sb("ident", [P, P])
        ident_bf = sb("ident_bf", [P, P], bf16)
        mask_bf = sb("mask_bf", [P, P], bf16)
        ln_col = sb("ln_col", [P, 2])
        b0_row = sb("b0_row", [P, E])
        router_sb = sb("router_sb", [P, EXPERTS])
        down_sb = sb("down_sb", [P, P])
        up_sb = sb("up_sb", [P, E])
        minus_half = sb("minus_half", [P, QB])
        earlier = sb("earlier", [P, EXPERTS, EXPERTS])
        own = sb("own", [P, EXPERTS])
        wt = sb("wt", [P, 3, P])
        bias_col = sb("bias_col", [P, 2])
        bv_row = sb("bv_row", [P, P])
        w0_sb = sb("w0_sb", [P, E])
        xnt = sb("xnt", [P, S])
        q_raw = sb("q_raw", [P, S])
        k_raw = sb("k_raw", [P, S])
        q_low = sb("q_low", [P, S], fp32r)
        stacks = [sb(f"stacks{i}", [P, 6, S], fp32r) for i in range(2)]
        QA, QBS, KHA, KHB, KLA, KLB = range(6)
        v_sb = [sb(f"v_sb{i}", [P, QB, P]) for i in range(2)]
        probs = [sb(f"probs{i}", [P, S]) for i in range(2)]
        turned = sb("turned", [P, 2 * QB * HALF + 2 * HB * HALF])
        turned0 = turned[:, 0:2 * QB * HALF].rearrange("p (h j q) -> p h j q", h=2, j=QB)
        turned1 = turned[:, 2 * QB * HALF:].rearrange("p (h j q) -> p h j q", h=2, j=HB)
        neg_max = sb("neg_max", [P, STEPS])
        sums = [sb(f"sums{i}", [P, 2, QB]) for i in range(2)]
        inv_sums = sb("inv_sums", [P, 2, QB])
        inv_row = sb("inv_row", [P, S])
        o_raw = sb("o_raw", [P, S])
        o_norm = sb("o_norm", [P, S])
        acc = sb("acc", [P, T // P, E])
        gate = sb("gate", [P, 8, EXPERTS])
        rank8 = sb("rank8", [P, 2, EXPERTS, EXPERTS])
        first_tok = sb("first_tok", [P, P])

        x_a = sb("x_a", [P, QB, E])
        y_a = sb("y_a", [P, QB, E])
        z_a = sb("z_a", [P, QB, E])
        zt_a = sb("zt_a", [P, S])
        x_b = sb("x_b", [P, QB, E])
        res_b = sb("res_b", [P, QB, E])
        u_b = sb("u_b", [P, QB, E])
        u_t = sb("u_t", [P, S])
        dg_t = sb("dg_t", [P, S])
        stats = [sb(f"stats{i}", [P, QB, 6]) for i in range(5)]
        moments = [sb(f"moments{i}", [P, 7, QB]) for i in range(5)]

        sc = [ps(f"sc{i}", [P, S]) for i in range(2)]
        tp = [ps(f"tp{i}", [P, 512]) for i in range(2)]
        po = ps("po", [P, HALF])
        pp = ps("pp", [P, 512])

        s_small, s_const = sem("s_small"), sem("s_const")
        s_xa, s_xb = sem("s_xa"), sem("s_xb")
        s_da, s_db = sem("s_da"), sem("s_db")
        s_va, s_vb = sem("s_va"), sem("s_vb")
        s_pa, s_pb = sem("s_pa"), sem("s_pb")
        s_z = sem("s_z")
        s_zt = sem("s_zt")
        s_xnt = sem("s_xnt")
        s_xnt_out = sem("s_xnt_out")
        s_y = sem("s_y")
        s_r = sem("s_r")
        s_x1 = sem("s_x1")
        s_u = sem("s_u")
        s_ut = sem("s_ut")
        s_ut_out = sem("s_ut_out")
        s_first = sem("s_first")
        s_logit = sem("s_logit")
        s_lcopy = sem("s_lcopy")
        s_lm = sem("s_lm")
        s_ge = sem("s_ge")
        s_gate = sem("s_gate")
        s_down = sem("s_down")
        s_dg = sem("s_dg")
        s_up = sem("s_up")
        s_f = sem("s_f")
        s_n3 = sem("s_n3")
        s_res = sem("s_res")
        s_out = sem("s_out")
        s_w = sem("s_w")
        s_w0 = sem("s_w0")
        s_qk = sem("s_qk")
        s_q_out = sem("s_q_out")
        s_k_out = sem("s_k_out")
        s_q_high = sem("s_q_high")
        s_k_high = sem("s_k_high")
        s_cut = sem("s_cut")
        s_q_cut = sem("s_q_cut")
        s_k_cut = sem("s_k_cut")
        s_stack = sem("s_stack")
        s_v = sem("s_v")
        s_v_out = sem("s_v_out")
        s_score = sem("s_score")
        s_max = sem("s_max")
        s_exp = sem("s_exp")
        s_turn = sem("s_turn")
        s_ta, s_td = sem("s_ta"), sem("s_td")
        s_pv0, s_pv1 = sem("s_pv0"), sem("s_pv1")
        s_o_out = sem("s_o_out")
        s_inv = sem("s_inv")
        s_inv_out = sem("s_inv_out")
        s_inv_row = sem("s_inv_row")
        s_norm = sem("s_norm")
        s_w0p = sem("s_w0p")
        s_acc = sem("s_acc")

        block = ctx.enter_context(nc.Block())

        def pairs(eng, body):
            def sided(c, after, before):
                for i in range(4):
                    body(c * PAIRS + 1 + i, (1 + i) % 2, False, False, (i, c, after, before))

            def plain(c, count):
                with eng.Fori(0, count) as t:
                    body(c * PAIRS + t * 2 + 5, 1, False, False, None)
                    body(c * PAIRS + t * 2 + 6, 0, False, False, None)

            body(0, 0, True, False, None)
            sided(0, False, True)
            plain(0, (PAIRS - 4) // 2)
            with eng.Fori(1, B - 1) as c:
                sided(c, True, True)
                plain(c, (PAIRS - 4) // 2)
            sided(B - 1, True, False)
            plain(B - 1, (PAIRS - 6) // 2)
            body(N - 1, 1, False, True, None)

        def reach(eng, semaphore, count):
            if not (isinstance(count, int) and count == 0):
                eng.wait_ge(semaphore, count)

        @block.sync
        def _(sp):
            def load_x(dst, c, done):
                sp.dma_start(dst[:], x[bass.ds(c * S, S), :].rearrange("(t p) e -> p t e", p=P)).then_inc(done, 16)

            def load_weights(n, with_x=True):
                p, b, column = n % PAIRS, (n // PAIRS) * S, (n % PAIRS) * P
                sp.dma_start(wt[:].rearrange("p a c -> p (a c)"),
                             w_pairs[bass.ds(p, 1), :, :].rearrange("o p n -> (o p) n")).then_inc(s_w, 16)
                sp.dma_start(bias_col[:], qk_bias[bass.ds(p, 1), :, :].rearrange("o p n -> (o p) n")).then_inc(s_w, 16)
                sp.dma_start(bv_row[:], bv[0:1, bass.ds(column, P)].to_broadcast([P, P])).then_inc(s_w, 16)
                if with_x:
                    sp.dma_start(xnt[:], xnt_dram[:, bass.ds(b, S)]).then_inc(s_w, 16)

            def build_stacks(n, parity):
                st, q_lo = stacks[parity][:].bitcast(fp32), q_low[:].bitcast(fp32)
                sp.wait_ge(s_q_cut, n + 1)
                sp.dma_start(st[D:P, QA, :], q_lo[0:D, :]).then_inc(s_stack, 16)
                sp.dma_start(st[0:D, QBS, :], q_lo[D:P, :]).then_inc(s_stack, 16)
                sp.wait_ge(s_k_cut, n + 1)
                for k in (KHA, KLA):
                    sp.dma_start(st[D:P, k, :], st[0:D, k, :]).then_inc(s_stack, 16)
                for k in (KHB, KLB):
                    sp.dma_start(st[0:D, k, :], st[D:P, k, :]).then_inc(s_stack, 16)

            def spread_sums(g):
                sp.wait_ge(s_inv, g + 1)
                sp.dma_start(sums_dram.rearrange("h p i -> p h i"), inv_sums[:]).then_inc(s_inv_out, 16)
                sp.wait_ge(s_inv_out, 16 * (g + 1))
                for h in range(2):
                    sp.dma_start(inv_row[h * D:(h + 1) * D, :],
                                 sums_dram[h:h + 1, :, :].rearrange("o p i -> o (p i)").to_broadcast([D, S])
                                 ).then_inc(s_inv_row, 16)

            def store_xnt(c, src):
                sp.dma_start(xnt_dram[:, bass.ds(c * S, S)], src[:]).then_inc(s_xnt_out, 16)

            def store_result(c):
                sp.wait_ge(s_res, c + 1)
                sp.dma_start(out[bass.ds(c * S, S), :].rearrange("(t p) e -> p t e", p=P), res_b[:]).then_inc(s_out, 16)

            load_x(x_a, 0, s_xa)
            for dst, src in ((ln_col[:], ln_gb), (router_sb[:], router_t), (down_sb[:], down_t),
                             (up_sb[:], up_r), (b0_row[:], b0.to_broadcast([P, E]))):
                sp.dma_start(dst, src).then_inc(s_small, 16)
            load_weights(0, False)
            sp.wait_ge(s_xnt, 2)
            store_xnt(0, xnt)
            build_stacks(0, 0)
            sp.wait_ge(s_v_out, 2)
            sp.wait_ge(s_k_out, 2)
            sp.wait_ge(s_xnt_out, 16)
            load_weights(1)

            def pair(g, parity, first, last, side):
                i, c, after, before = side or (None, 0, False, False)
                if i == 0 and after:
                    load_x(x_b, c - 1, s_xb)
                if i == 0 and before:
                    load_x(x_a, c + 1, s_xa)
                if i == 3 and before:
                    sp.wait_ge(s_xnt, 2 * c + 4)
                if not first:
                    spread_sums(g - 1)
                if i == 3 and before:
                    store_xnt(c + 1, zt_a)
                if i == 3 and after:
                    store_result(c - 1)
                if not last:
                    build_stacks(g + 1, 1 - parity)
                    sp.wait_ge(s_v_out, 2 * g + 4)
                    sp.wait_ge(s_k_out, 2 * g + 4)
                    load_weights((g + 2) % N)
                if i == 3 and before:
                    sp.wait_ge(s_xnt_out, 16 * (c + 2))
                if not first:
                    sp.wait_ge(s_acc, 2 * g)
                sp.dma_start(w0_sb[:], w0[bass.ds((g % PAIRS) * P, P), :]).then_inc(s_w0, 16)

            pairs(sp, pair)
            load_x(x_b, B - 1, s_xb)
            spread_sums(N - 1)
            store_result(B - 1)
            sp.wait_ge(s_out, 16 * B)
            sp.wait_ge(s_w, 16 * W_DMAS * (N + 1) - 16)

        @block.gpsimd
        def _(pool):
            nc.gpsimd.memset(minus_half[:], -0.5)
            nc.gpsimd.memset(ident[:], 0.0)
            nc.gpsimd.memset(ident_bf[:], 0.0)
            nc.gpsimd.memset(mask_bf[:], 0.0)
            nc.gpsimd.memset(earlier[:], 1.0)
            nc.gpsimd.memset(own[:], 1.0).then_inc(s_const, 1)
            pool.wait_ge(s_const, 1)
            nc.gpsimd.affine_select(out=ident[:], in_=ident[:], compare_op=ALU.not_equal, fill=1.0, base=0,
                                    pattern=[[-1, P]], channel_multiplier=1)
            nc.gpsimd.affine_select(out=ident_bf[:], in_=ident_bf[:], compare_op=ALU.not_equal, fill=1.0, base=0,
                                    pattern=[[-1, P]], channel_multiplier=1)
            nc.gpsimd.affine_select(out=mask_bf[:], in_=mask_bf[:], compare_op=ALU.is_ge, fill=MASKED, base=0,
                                    pattern=[[1, P]], channel_multiplier=-1)
            nc.gpsimd.affine_select(out=earlier[:], in_=earlier[:], compare_op=ALU.is_ge, fill=0.0, base=-1,
                                    pattern=[[1, EXPERTS], [-1, EXPERTS]], channel_multiplier=0)
            nc.gpsimd.affine_select(out=own[:], in_=own[:], compare_op=ALU.is_ge, fill=0.0, base=0,
                                    pattern=[[-RANK, EXPERTS]], channel_multiplier=1).then_inc(s_const, 1)
            pool.wait_ge(s_const, 2)
            nc.gpsimd.affine_select(out=own[:], in_=own[:], compare_op=ALU.is_ge, fill=0.0, base=RANK - 1,
                                    pattern=[[RANK, EXPERTS]], channel_multiplier=-1).then_inc(s_const, 1)

            def inverse_roots(norm, c):
                made, done, count = (s_va, s_pa, c * 2 + 1 + norm) if norm < 2 else (s_vb, s_pb, c * 3 + norm - 1)
                pool.wait_ge(made, count)
                m = moments[norm]
                nc.gpsimd.tensor_tensor(m[:, 6, :], m[:, 5, :], minus_half[:], ALU.pow).then_inc(done, 1)
                pool.wait_ge(done, count)

            def start_acc(c):
                pool.wait_ge(s_z, c + 1)
                nc.gpsimd.tensor_tensor(acc[:, bass.ds(c * QB, QB), :], y_a[:],
                                        b0_row[:].unsqueeze(1).to_broadcast([P, QB, E]), ALU.add).then_inc(s_y, 1)
                pool.wait_ge(s_y, c + 1)

            def add_x(c):
                pool.wait_ge(s_xb, 16 * (c + 1))
                pool.wait_ge(s_r, c + 1)
                nc.gpsimd.tensor_tensor(x_b[:], x_b[:], res_b[:], ALU.add).then_inc(s_x1, 1)
                pool.wait_ge(s_x1, c + 1)

            def add_x1(c):
                pool.wait_ge(s_n3, c + 1)
                nc.gpsimd.tensor_tensor(res_b[:], res_b[:], x_b[:], ALU.add).then_inc(s_res, 1)
                pool.wait_ge(s_res, c + 1)

            inverse_roots(0, 0)
            inverse_roots(1, 0)
            start_acc(0)

            def low(dst, src, hi):
                return nc.gpsimd.tensor_tensor(dst, src, hi.bitcast(fp32), ALU.subtract)

            def cut_q(n, parity, first):
                st = stacks[parity]
                pool.wait_ge(s_q_high, n + 1)
                if not first:
                    pool.wait_ge(s_k_cut, n)
                    pool.wait_ge(s_stack, 16 * STACK_DMAS * n)
                low(q_low[0:D, :], q_raw[0:D, :], st[0:D, QA, :]).then_inc(s_cut, 1)
                pool.wait_ge(s_cut, 2 * n + 1)
                low(q_low[D:P, :], q_raw[D:P, :], st[D:P, QBS, :]).then_inc(s_q_cut, 1)

            def cut_k(n, parity):
                st = stacks[parity]
                if isinstance(n, int) and n <= 1:
                    pool.wait_ge(s_q_cut, n + 1)
                else:
                    reach(pool, s_norm, 2 * (n - 1))
                pool.wait_ge(s_k_high, n + 1)
                low(st[0:D, KLA, :], k_raw[0:D, :], st[0:D, KHA, :]).then_inc(s_cut, 1)
                pool.wait_ge(s_cut, 2 * n + 2)
                low(st[D:P, KLB, :], k_raw[D:P, :], st[D:P, KHB, :]).then_inc(s_k_cut, 1)

            def normalise(g, before, count):
                inv = inv_row[:].rearrange("p (q i) -> p i q", i=QB)
                pool.wait_ge(before, count)
                pool.wait_ge(s_inv_row, 32 * (g + 1))
                reach(pool, s_w0p, 2 * g)
                for half in range(2):
                    pool.wait_ge(s_o_out, 2 * g + 1 + half)
                    if half:
                        pool.wait_ge(s_norm, 2 * g + 1)
                    q = slice(half * HALF, (half + 1) * HALF)
                    nc.gpsimd.tensor_tensor(o_norm[:, q].rearrange("p (i q) -> p i q", q=P),
                                            o_raw[:, q].rearrange("p (i q) -> p i q", q=P),
                                            inv[:, half * HB:(half + 1) * HB, :], ALU.mult).then_inc(s_norm, 1)

            cut_q(0, 0, True)
            cut_k(0, 0)

            def pair(g, parity, first, last, side):
                i, c, after, before = side or (None, 0, False, False)
                if not last:
                    if i == 2 and before:
                        pool.wait_ge(s_k_cut, g + 1)
                        inverse_roots(1, c + 1)
                    cut_q(g + 1, 1 - parity, False)
                if (i == 0 and after) or (i in (1, 2) and before):
                    pool.wait_ge(s_q_cut, g + 2)
                if i == 0 and after:
                    inverse_roots(2, c - 1)
                    add_x(c - 1)
                if i == 1 and before:
                    inverse_roots(0, c + 1)
                if i == 2 and before:
                    start_acc(c + 1)
                if not first:
                    normalise(g - 1, *((s_k_cut, N) if last else (s_q_cut, g + 2)))
                if not last:
                    cut_k(g + 1, 1 - parity)
                if i in (0, 2) and after:
                    pool.wait_ge(s_k_cut, g + 2)
                    if i == 0:
                        inverse_roots(3, c - 1)
                    else:
                        inverse_roots(4, c - 1)
                        add_x1(c - 1)

            pairs(pool, pair)
            normalise(N - 1, s_norm, 2 * (N - 1))
            pool.wait_ge(s_norm, 2 * N)
            inverse_roots(2, B - 1)
            add_x(B - 1)
            inverse_roots(3, B - 1)
            inverse_roots(4, B - 1)
            add_x1(B - 1)

        @block.tensor
        def _(pe):
            def turn_four(src, a):
                for j in range(4):
                    last = nc.tensor.transpose(pp[:, j * P:(j + 1) * P], src[:, 4 * a + j, :], ident[:])
                return last

            def turn_z(c, a):
                pe.wait_ge(s_z, c + 1)
                turn_four(z_a, a).then_inc(s_zt, 1)
                return s_xnt, c * 2 + a + 1

            def turn_u(c, a):
                pe.wait_ge(s_u, c + 1)
                turn_four(u_b, a).then_inc(s_ut, 1)
                return s_ut_out, c * 2 + a + 1

            def logits(c):
                pe.wait_ge(s_first, c + 1)
                nc.tensor.matmul(pp[:, 0:EXPERTS], first_tok[:], router_sb[:], start=True, stop=True).then_inc(s_logit, 1)
                return s_lcopy, c + 1

            def project_down(c, a):
                pe.wait_ge(s_ut_out, c * 2 + a + 1)
                nc.tensor.matmul(pp[:], down_sb[:], u_t[:, a * 512:(a + 1) * 512], start=True,
                                 stop=True).then_inc(s_down, 1)
                return s_dg, c * 2 + a + 1

            def project_up(c, a):
                pe.wait_ge(s_dg, c * 2 + a + 1)
                for j in range(4):
                    t = 4 * a + j
                    last = nc.tensor.matmul(pp[:, j * P:(j + 1) * P], dg_t[:, t * P:(t + 1) * P], up_sb[:],
                                            start=True, stop=True)
                last.then_inc(s_up, 1)
                return s_f, c * 2 + a + 1

            pe.wait_ge(s_const, 3)
            pe.wait_ge(s_small, 16 * 5)
            pe.wait_ge(*turn_z(0, 0))
            pe.wait_ge(*turn_z(0, 1))

            def project(n, part):
                if part == 0:
                    pe.wait_ge(s_w, 16 * W_DMAS * (n + 1) - 16)
                c = part % 2
                nc.tensor.matmul(pp[:], wt[:, part // 2, :], xnt[:, c * HALF:(c + 1) * HALF],
                                 start=True, stop=True).then_inc(s_qk, 1)

            def project_v(n, c):
                for j in range(4):
                    t = 4 * c + j
                    last = nc.tensor.matmul(pp[:, j * P:(j + 1) * P], xnt[:, t * P:(t + 1) * P], wt[:, 2, :],
                                            start=True, stop=True)
                last.then_inc(s_v, 1)

            def scores(g, parity, k):
                i, h = k // 2, k % 2
                st = stacks[parity]
                width = (QB - i) * P
                for o in range(0, width, 512):
                    w = min(512, width - o)
                    dst = sc[k % 2][:, o:o + w]
                    q = st[:, QA + h, i * P:(i + 1) * P]
                    keys = slice(i * P + o, i * P + o + w)
                    nc.tensor.matmul(dst, q, st[:, KHA + h, keys], start=True, stop=False)
                    last = nc.tensor.matmul(dst, q, st[:, KLA + h, keys], start=False, stop=(o > 0))
                    if o == 0:
                        last = nc.tensor.matmul(dst[:, 0:P], ident_bf[:], mask_bf[:], start=False, stop=True)
                last.then_inc(s_score, 1)

            def turn(g, k):
                pe.wait_ge(s_exp, STEPS * g + k + 1)
                for n, (c0, m) in enumerate(TURNS[k]):
                    t = TURN0[k] + n
                    if t >= 2 or not (isinstance(g, int) and g == 0):
                        pe.wait_ge((s_ta, s_td)[t % 2], EVACS * g + t // 2)
                    for j in range(m):
                        last = nc.tensor.transpose(tp[t % 2][:, j * P:(j + 1) * P],
                                                   probs[k % 2][:, (c0 + j) * P:(c0 + j + 1) * P], ident[:])
                    last.then_inc(s_turn, 1)

            def outputs(g, parity, half, blocks):
                for j in blocks:
                    w = min(HB, j + 1 - half * HB) * P
                    for h in range(2):
                        src = (turned0 if half == 0 else turned1)[:, h, j - half * HB, 0:w]
                        last = nc.tensor.matmul(po[h * D:(h + 1) * D, 0:w], v_sb[parity][:, j, h * D:(h + 1) * D],
                                                src, start=(j == QB - 1), stop=(j == half * HB))
                if j == half * HB:
                    last.then_inc((s_pv0, s_pv1)[half], 1)

            def project_out(g, c):
                pe.wait_ge(s_norm, 2 * g + 1 + c)
                if c == 0:
                    pe.wait_ge(s_w0, 16 * (g + 1))
                for j in range(4):
                    t = 4 * c + j
                    last = nc.tensor.matmul(pp[:, j * P:(j + 1) * P], o_norm[:, t * P:(t + 1) * P], w0_sb[:],
                                            start=True, stop=True)
                last.then_inc(s_w0p, 1)

            project(0, 0)
            pe.wait_ge(s_q_out, 1)
            project(0, 1)
            pe.wait_ge(s_q_out, 2)
            project(0, 2)
            pe.wait_ge(s_k_out, 1)
            project(0, 3)
            pe.wait_ge(s_k_out, 2)
            project_v(0, 0)
            pe.wait_ge(s_v_out, 1)
            project_v(0, 1)

            AFTER = {1: {2: (turn_u, 0), 4: (turn_u, 1), 6: (logits,), 9: (project_down, 0), 11: (project_down, 1),
                         12: (project_up, 0), 13: (project_up, 1)}}
            BEFORE = {2: {4: (turn_z, 0), 6: (turn_z, 1)}}

            def pair(g, parity, first, last, side):
                n = g + 1
                i, c, after, before = side or (None, 0, False, False)
                busy = []

                def pp_after(semaphore, count):
                    if busy:
                        pe.wait_ge(*busy.pop())
                    else:
                        reach(pe, semaphore, count)

                before_step = {2: (s_q_out, 2 * n + 2), 4: (s_k_out, 2 * n + 1), 6: (s_k_out, 2 * n + 2),
                               9: (s_v_out, 2 * n + 2), 11: (s_acc, 2 * g - 1), 12: (s_acc, 2 * g - 1),
                               13: (s_acc, 2 * g - 1)}

                for k in range(STEPS):
                    if k == 0:
                        pe.wait_ge(s_stack, 16 * STACK_DMAS * (g + 1))
                    if k > 1 or not first:
                        pe.wait_ge(s_exp, STEPS * g + k - 1)
                    scores(g, parity, k)
                    if k == 0 and not last:
                        pp_after(*((s_v_out, 2) if first else (s_acc, 2 * (g - 1))))
                        project(n, 0)
                    if k == 1 and not last:
                        pp_after(s_q_out, 2 * n + 1)
                        project(n, 1)
                    if k == 2 and not first:
                        pe.wait_ge(s_ta, EVACS * g)
                        pe.wait_ge(s_td, EVACS * g)
                        pe.wait_ge(s_o_out, 2 * g - 1)
                        outputs(g - 1, 1 - parity, 1, (7,))
                    if k == 3 and not last:
                        pp_after(s_q_out, 2 * n + 2)
                        project(n, 2)
                    if k == 4 and not first:
                        outputs(g - 1, 1 - parity, 1, (6,))
                    if k == 5 and not last:
                        pp_after(s_k_out, 2 * n + 1)
                        project(n, 3)
                    if k == 6 and not first:
                        outputs(g - 1, 1 - parity, 1, (5, 4))
                    if k == 7 and not last:
                        pp_after(s_k_out, 2 * n + 2)
                        project_v(n, 0)
                    if k == 8 and not last:
                        pp_after(s_v_out, 2 * n + 1)
                        project_v(n, 1)
                    if k == 9:
                        pe.wait_ge(s_ta, EVACS * g + EVACS0)
                        pe.wait_ge(s_td, EVACS * g + EVACS0)
                        if not first:
                            pe.wait_ge(s_o_out, 2 * g)
                        outputs(g, parity, 0, (7,))
                    if k == 10 and not first:
                        pp_after(s_v_out, 2 * (g + 1) if last else 2 * n + 2)
                        project_out(g - 1, 0)
                    if 11 <= k <= 13:
                        outputs(g, parity, 0, (17 - k,))
                    if k == 14:
                        outputs(g, parity, 0, (3, 2, 1, 0))
                    if k == 15 and not first:
                        pp_after(s_acc, 2 * (g - 1) + 1)
                        project_out(g - 1, 1)
                    for wanted, table, b in ((after, AFTER, c - 1), (before, BEFORE, c + 1)):
                        if wanted and k in table.get(i, {}):
                            use, *part = table[i][k]
                            pp_after(*before_step[k])
                            busy.append(use(b, *part))
                    if k:
                        turn(g, k - 1)
                    elif not first:
                        turn(g - 1, STEPS - 1)

            pairs(pe, pair)
            g = N - 1
            turn(g, STEPS - 1)
            pe.wait_ge(s_ta, EVACS * N)
            pe.wait_ge(s_td, EVACS * N)
            pe.wait_ge(s_o_out, 2 * g + 1)
            outputs(g, 1, 1, (7, 6, 5, 4))
            pe.wait_ge(s_acc, 2 * g)
            project_out(g, 0)
            pe.wait_ge(s_acc, 2 * g + 1)
            project_out(g, 1)
            pe.wait_ge(s_acc, 2 * N)
            for a in range(2):
                pe.wait_ge(*turn_u(B - 1, a))
            pe.wait_ge(*logits(B - 1))
            for a in range(2):
                pe.wait_ge(*project_down(B - 1, a))
            for a in range(2):
                pe.wait_ge(*project_up(B - 1, a))

        @block.scalar
        def _(act):
            act.wait_ge(s_small, 16 * 5)

            def take_z(c, a, dst):
                act.wait_ge(s_zt, c * 2 + a + 1)
                nc.scalar.activation(dst[:, a * 512:(a + 1) * 512], pp[:], ACT.Identity,
                                     bias=ln_col[:, 1:2], scale=ln_col[:, 0:1]).then_inc(s_xnt, 1)

            def take_u(c, a):
                act.wait_ge(s_ut, c * 2 + a + 1)
                nc.scalar.copy(u_t[:, a * 512:(a + 1) * 512], pp[:]).then_inc(s_ut_out, 1)

            def spread_first(c):
                act.wait_ge(s_ut_out, c * 2 + 1)
                nc.scalar.copy(first_tok[:], u_t[:, 0:1].to_broadcast([P, P])).then_inc(s_first, 1)

            def exp_logits(c):
                act.wait_ge(s_lm, c + 1)
                nc.scalar.activation(gate[:, 2, :], gate[:, 0, :], ACT.Exp, bias=gate[:, 1, 0:1]).then_inc(s_ge, 1)

            def take_down(c, a):
                act.wait_ge(s_gate, c + 1)
                act.wait_ge(s_down, c * 2 + a + 1)
                nc.scalar.activation(dg_t[:, a * 512:(a + 1) * 512], pp[:], ACT.Copy,
                                     scale=gate[:, 7, 0:1]).then_inc(s_dg, 1)

            take_z(0, 0, xnt)
            take_z(0, 1, xnt)

            def take_k(n, c, wait):
                act.wait_ge(s_qk, 4 * n + 3 + c)
                if wait:
                    act.wait_ge(s_k_cut, n)
                nc.scalar.activation(k_raw[:, c * HALF:(c + 1) * HALF], pp[:], ACT.Identity,
                                     bias=bias_col[:, 1:2]).then_inc(s_k_out, 1)

            def take_o(g, half):
                act.wait_ge((s_pv0, s_pv1)[half], g + 1)
                if not (isinstance(g, int) and g == 0):
                    act.wait_ge(s_norm, 2 * (g - 1) + 1 + half)
                nc.scalar.copy(o_raw[:, half * HALF:(half + 1) * HALF], po[:]).then_inc(s_o_out, 1)

            def take_turn(g, k):
                i, h = k // 2, k % 2
                for n, (c0, m) in enumerate(TURNS[k]):
                    t = TURN0[k] + n
                    if t % 2:
                        continue
                    reach(act, s_pv0 if i < HB else s_pv1, g)
                    act.wait_ge(s_turn, NTURN * g + t + 1)
                    dst, at = (turned0, 0) if i < HB else (turned1, HB)
                    nc.scalar.copy(dst[:, h, i + c0 - at:i + c0 - at + m, (i - at) * P:(i - at + 1) * P],
                                   tp[0][:, 0:m * P].rearrange("p (j q) -> p j q", q=P)).then_inc(s_ta, 1)

            act.wait_ge(s_w, 16 * W_DMAS - 16)
            take_k(0, 0, False)
            take_k(0, 1, False)

            AFTER = {1: {2: lambda b: (take_u(b, 0), spread_first(b)), 4: lambda b: take_u(b, 1),
                         7: exp_logits, 9: lambda b: take_down(b, 0), 11: lambda b: take_down(b, 1)}}
            BEFORE = {2: {4: lambda b: take_z(b, 0, zt_a), 6: lambda b: take_z(b, 1, zt_a)}}

            def pair(g, parity, first, last, side):
                stage, c, after, before = side or (None, 0, False, False)
                for k in range(STEPS):
                    i, h = k // 2, k % 2
                    width = (QB - i) * P
                    act.wait_ge(s_max, STEPS * g + k + 1)
                    if k == 0 and not first:
                        act.wait_ge(s_inv, g)
                    nc.scalar.activation(probs[k % 2][:, 0:width], sc[k % 2][:, 0:width], ACT.Exp,
                                         bias=neg_max[:, k:k + 1],
                                         accum_out=sums[parity][:, h, i:i + 1]).then_inc(s_exp, 1)
                    if k == 3 and not last:
                        take_k(g + 1, 0, True)
                    if k == 5 and not last:
                        take_k(g + 1, 1, True)
                    if k == 6 and not first:
                        take_o(g - 1, 1)
                    if k == 14:
                        take_o(g, 0)
                    for wanted, table, b in ((after, AFTER, c - 1), (before, BEFORE, c + 1)):
                        if wanted and k in table.get(stage, {}):
                            table[stage][k](b)
                    if k:
                        take_turn(g, k - 1)
                    elif not first:
                        take_turn(g - 1, STEPS - 1)

            pairs(act, pair)
            take_turn(N - 1, STEPS - 1)
            take_o(N - 1, 1)

            b = B - 1
            take_u(b, 0)
            spread_first(b)
            take_u(b, 1)
            exp_logits(b)
            take_down(b, 0)
            take_down(b, 1)

        @block.vector
        def _(dve):
            links = {s_da: 0, s_db: 0}

            def link(ins, semaphore, c):
                per_batch = A_LINKS if semaphore is s_da else B_LINKS
                links[semaphore] = links[semaphore] % per_batch + 1
                ins.then_inc(semaphore, 1)
                dve.wait_ge(semaphore, c * per_batch + links[semaphore])

            def chain_of(norm):
                return s_da if norm < 2 else s_db

            def norm_stats(norm, src, c, a):
                for t in range(4 * a, 4 * a + 4):
                    last = nc.vector.bn_stats(stats[norm][:, t, :], src[:, t, :])
                if a:
                    link(last, chain_of(norm), c)

            def norm_moments(norm, c):
                m, by = moments[norm], chain_of(norm)
                me, qe, mo, qo = (stats[norm][:, :, a:a + 1].rearrange("p t o -> p (t o)") for a in (1, 2, 4, 5))
                nc.vector.tensor_tensor(m[:, 0, :], me, mo, ALU.add)
                nc.vector.tensor_tensor(m[:, 1, :], me, mo, ALU.subtract)
                link(nc.vector.tensor_tensor(m[:, 2, :], qe, qo, ALU.add), by, c)
                nc.vector.tensor_scalar(m[:, 3, :], m[:, 0, :], 0.5, None, ALU.mult)
                link(nc.vector.tensor_tensor(m[:, 4, :], m[:, 1, :], m[:, 1, :], ALU.mult), by, c)
                link(nc.vector.scalar_tensor_tensor(out=m[:, 4, :], in0=m[:, 4, :], scalar=E / 4,
                                                    in1=m[:, 2, :], op0=ALU.mult, op1=ALU.add), by, c)
                nc.vector.tensor_scalar(m[:, 5, :], m[:, 4, :], 1.0 / E, EPS, ALU.mult,
                                        ALU.add).then_inc(s_va if norm < 2 else s_vb, 1)

            def norm_apply(norm, dst, src, c):
                dve.wait_ge(*((s_pa, c * 2 + 1 + norm) if norm < 2 else (s_pb, c * 3 + norm - 1)))
                m = moments[norm]
                for t in range(QB):
                    last = nc.vector.tensor_scalar(dst[:, t, :], src[:, t, :], m[:, 3, t:t + 1], m[:, 6, t:t + 1],
                                                   ALU.subtract, ALU.mult)
                return last

            def acc_of(c):
                return acc[:, bass.ds(c * QB, QB), :]

            def a1_stats(c, a):
                if a == 0:
                    dve.wait_ge(s_xa, 16 * (c + 1))
                norm_stats(0, x_a, c, a)

            def a1_apply(c):
                link(norm_apply(0, y_a, x_a, c), s_da, c)

            def a2_apply(c):
                norm_apply(1, z_a, y_a, c).then_inc(s_z, 1)

            def b1_apply(c):
                norm_apply(2, res_b, acc_of(c), c).then_inc(s_r, 1)

            def b2_stats(c, a):
                if a == 0:
                    dve.wait_ge(s_x1, c + 1)
                norm_stats(3, x_b, c, a)

            def b2_apply(c):
                norm_apply(3, u_b, x_b, c).then_inc(s_u, 1)

            def take_logits(c):
                dve.wait_ge(s_logit, c + 1)
                nc.vector.tensor_copy(gate[:, 0, :], pp[:, 0:EXPERTS]).then_inc(s_lcopy, 1)
                dve.wait_ge(s_lcopy, c + 1)
                nc.vector.tensor_reduce(gate[:, 1, 0:1], gate[:, 0, :], AX.X, ALU.max, negate=True).then_inc(s_lm, 1)

            def rank_logits(c):
                mine = gate[:, 0, :].unsqueeze(2).to_broadcast([P, EXPERTS, EXPERTS])
                others = gate[:, 0, :].unsqueeze(1).to_broadcast([P, EXPERTS, EXPERTS])
                nc.vector.tensor_tensor(rank8[:, 1], others, mine, ALU.is_gt)
                link(nc.vector.tensor_tensor(rank8[:, 0], others, mine, ALU.is_equal), s_db, c)
                link(nc.vector.tensor_tensor(rank8[:, 0], rank8[:, 0], earlier[:], ALU.mult), s_db, c)
                link(nc.vector.tensor_tensor(rank8[:, 0], rank8[:, 0], rank8[:, 1], ALU.add), s_db, c)
                link(nc.vector.tensor_reduce(gate[:, 3, :], rank8[:, 0], AX.X, ALU.add), s_db, c)
                link(nc.vector.tensor_scalar(gate[:, 3, :], gate[:, 3, :], 2.0, None, ALU.is_lt), s_db, c)

            def make_gate(c):
                dve.wait_ge(s_ge, c + 1)
                link(nc.vector.tensor_tensor(gate[:, 4, :], gate[:, 2, :], gate[:, 3, :], ALU.mult), s_db, c)
                link(nc.vector.tensor_tensor(gate[:, 5, :], gate[:, 4, :], own[:], ALU.mult), s_db, c)
                nc.vector.tensor_reduce(gate[:, 6, 1:2], gate[:, 5, :], AX.X, ALU.add)
                link(nc.vector.tensor_reduce(gate[:, 6, 0:1], gate[:, 4, :], AX.X, ALU.add), s_db, c)
                link(nc.vector.reciprocal(gate[:, 6, 2:3], gate[:, 6, 0:1]), s_db, c)
                nc.vector.tensor_tensor(gate[:, 7, 0:1], gate[:, 6, 1:2], gate[:, 6, 2:3],
                                        ALU.mult).then_inc(s_gate, 1)

            def take_up(c, a):
                dve.wait_ge(s_up, c * 2 + a + 1)
                f = u_b[:, 4 * a:4 * a + 4, :]
                nc.vector.tensor_tensor(f, pp[:].rearrange("p (j e) -> p j e", e=E), f, ALU.add).then_inc(s_f, 1)

            def b3_stats(c, a):
                dve.wait_ge(s_f, c * 2 + a + 1)
                norm_stats(4, u_b, c, a)

            def b3_apply(c):
                norm_apply(4, res_b, u_b, c).then_inc(s_n3, 1)

            AFTER = {0: {0: lambda b: norm_stats(2, acc_of(b), b, 0), 1: lambda b: norm_stats(2, acc_of(b), b, 1),
                         3: lambda b: norm_moments(2, b), 5: b1_apply,
                         9: lambda b: b2_stats(b, 0), 10: lambda b: b2_stats(b, 1), 11: lambda b: norm_moments(3, b),
                         14: b2_apply},
                     1: {6: take_logits, 7: rank_logits, 8: make_gate, 12: lambda b: take_up(b, 0),
                         13: lambda b: take_up(b, 1)},
                     2: {8: lambda b: b3_stats(b, 0), 9: lambda b: b3_stats(b, 1), 10: lambda b: norm_moments(4, b),
                         13: b3_apply}}
            BEFORE = {1: {0: lambda b: a1_stats(b, 0), 1: lambda b: a1_stats(b, 1), 3: lambda b: norm_moments(0, b),
                          5: a1_apply, 14: lambda b: norm_stats(1, y_a, b, 0), 15: lambda b: norm_stats(1, y_a, b, 1)},
                      2: {0: lambda b: norm_moments(1, b), 3: a2_apply}}

            def in_turn(tables, c):
                for table in tables:
                    for step in sorted(table):
                        table[step](c)

            dve.wait_ge(s_small, 16 * 5)
            dve.wait_ge(s_const, 3)
            in_turn((BEFORE[1], BEFORE[2]), 0)

            def take_q(n, c, wait):
                dve.wait_ge(s_qk, 4 * n + 1 + c)
                if wait:
                    dve.wait_ge(s_q_cut, n)
                nc.vector.tensor_scalar(q_raw[:, c * HALF:(c + 1) * HALF], pp[:], bias_col[:, 0:1], SCALE,
                                        ALU.add, ALU.mult).then_inc(s_q_out, 1)

            def high_q(n, parity):
                dve.wait_ge(s_q_out, 2 * n + 2)
                nc.vector.tensor_copy(stacks[parity][0:D, QA, :], q_raw[0:D, :])
                nc.vector.tensor_copy(stacks[parity][D:P, QBS, :], q_raw[D:P, :]).then_inc(s_q_high, 1)

            def high_k(n, parity):
                dve.wait_ge(s_k_out, 2 * n + 2)
                nc.vector.tensor_copy(stacks[parity][0:D, KHA, :], k_raw[0:D, :])
                nc.vector.tensor_copy(stacks[parity][D:P, KHB, :], k_raw[D:P, :]).then_inc(s_k_high, 1)

            def take_v(n, parity, c, wait):
                dve.wait_ge(s_v, 2 * n + 1 + c)
                if wait:
                    reach(dve, s_pv1, n - 1)
                nc.vector.tensor_tensor(v_sb[parity][:, 4 * c:4 * c + 4, :],
                                        pp[:].rearrange("p (j d) -> p j d", d=P),
                                        bv_row[:].unsqueeze(1).to_broadcast([P, 4, P]), ALU.add).then_inc(s_v_out, 1)

            def take_turn(g, k):
                i, h = k // 2, k % 2
                for n, (c0, m) in enumerate(TURNS[k]):
                    t = TURN0[k] + n
                    if t % 2 == 0:
                        continue
                    reach(dve, s_pv0 if i < HB else s_pv1, g)
                    dve.wait_ge(s_turn, NTURN * g + t + 1)
                    dst, at = (turned0, 0) if i < HB else (turned1, HB)
                    nc.vector.tensor_copy(dst[:, h, i + c0 - at:i + c0 - at + m, (i - at) * P:(i - at + 1) * P],
                                          tp[1][:, 0:m * P].rearrange("p (j q) -> p j q", q=P)).then_inc(s_td, 1)

            def invert_sums(g, parity):
                dve.wait_ge(s_exp, STEPS * (g + 1))
                reach(dve, s_inv_out, 16 * g)
                reach(dve, s_norm, 2 * g)
                nc.vector.reciprocal(inv_sums[:], sums[parity][:]).then_inc(s_inv, 1)

            def add_out(g, c):
                dve.wait_ge(s_w0p, 2 * g + 1 + c)
                reach(dve, s_acc, 2 * g)
                a = acc[:].rearrange("p t e -> p (t e)")[:, bass.ds((g // PAIRS) * (QB * E) + c * 512, 512)]
                nc.vector.tensor_tensor(a, pp[:], a, ALU.add).then_inc(s_acc, 1)

            dve.wait_ge(s_w, 16 * W_DMAS - 16)
            take_q(0, 0, False)
            take_q(0, 1, False)
            high_q(0, 0)
            high_k(0, 0)
            take_v(0, 0, 0, False)
            take_v(0, 0, 1, False)
            def pair(g, parity, first, last, side):
                stage, c, after, before = side or (None, 0, False, False)
                for k in range(STEPS):
                    i, h = k // 2, k % 2
                    width = (QB - i) * P
                    dve.wait_ge(s_score, STEPS * g + k + 1)
                    nc.vector.tensor_reduce(neg_max[:, k:k + 1], sc[k % 2][:, 0:width], AX.X, ALU.max,
                                            negate=True).then_inc(s_max, 1)
                    if k == 0 and not first:
                        invert_sums(g - 1, 1 - parity)
                    if k < 2 and not last:
                        take_q(g + 1, k, True)
                    if k == 2 and not last:
                        high_q(g + 1, 1 - parity)
                    if k == 6 and not last:
                        high_k(g + 1, 1 - parity)
                    if k in (7, 8) and not last:
                        take_v(g + 1, 1 - parity, k - 7, not first)
                    if k == 10 and not first:
                        add_out(g - 1, 0)
                    if k == 15 and not first:
                        add_out(g - 1, 1)
                    for wanted, table, b in ((after, AFTER, c - 1), (before, BEFORE, c + 1)):
                        if wanted and k in table.get(stage, {}):
                            table[stage][k](b)
                    if k:
                        take_turn(g, k - 1)
                    elif not first:
                        take_turn(g - 1, STEPS - 1)

            pairs(dve, pair)
            take_turn(N - 1, STEPS - 1)
            invert_sums(N - 1, 1)
            add_out(N - 1, 0)
            add_out(N - 1, 1)
            dve.wait_ge(s_acc, 2 * N)
            in_turn((AFTER[0], AFTER[1], AFTER[2]), B - 1)


def kernel(**inputs):
    import numpy as np
    import concourse.bacc as bacc
    from concourse import mybir as mb
    from concourse.bass_utils import run_bass_kernel_spmd as run

    def a(name):
        return np.asarray(inputs[name])

    x = a("L0_attn_x")
    pairs = a("L0_attn_wq").shape[1] // 128

    def by_pair(w):
        return w.reshape(w.shape[0], pairs, 128).transpose(1, 0, 2)

    down, up = a("L0_ffn_lora_down"), a("L0_ffn_lora_up")
    arrays = {
        "x": x.reshape(-1, x.shape[-1]),
        "ln_gb": np.stack([a("L0_attn_ln_g"), a("L0_attn_ln_b")], axis=1),
        "w_pairs": np.concatenate([by_pair(a(f"L0_attn_w{c}")) for c in "qkv"], axis=2),
        "qk_bias": np.stack([a("L0_attn_bq").reshape(pairs, 128), a("L0_attn_bk").reshape(pairs, 128)], axis=2),
        "bv": a("L0_attn_bv").reshape(1, -1),
        "w0": a("L0_attn_w0"),
        "b0": a("L0_attn_b0").reshape(1, -1),
        "router_t": a("L0_ffn_router_w").T,
        "down_t": down.reshape(-1, down.shape[-1]).T,
        "up_r": up.transpose(0, 2, 1).reshape(-1, up.shape[1]),
    }
    arrays = {n: np.ascontiguousarray(v) for n, v in arrays.items()}
    nc = bacc.Bacc("TRN2", target_bir_lowering=False, num_devices=1)
    f32 = mb.dt.float32
    args = {n: nc.dram_tensor(n, v.shape, mb.dt.from_np(v.dtype), kind="ExternalInput").ap() for n, v in arrays.items()}
    out = nc.dram_tensor("out", arrays["x"].shape, f32, kind="ExternalOutput").ap()
    xnt = nc.dram_tensor("xnt_dram", (128, arrays["x"].shape[0]), f32).ap()
    sums = nc.dram_tensor("sums_dram", (2, 128, 8), f32).ap()
    sandwich_kernel(nc, out=out, xnt_dram=xnt, sums_dram=sums, **args)
    r = run(nc, [arrays], core_ids=[0])
    return r.results[0]["out"].reshape(x.shape)
```

```python
import concourse.bass as bass
from concourse import mybir
from contextlib import ExitStack


def sandwich_kernel(nc, x, ln_gb, w_pairs, qk_bias, bv, w0, b0, router_t, down_t, up_r, out, sums_dram):
    fp32, fp32r, bf16 = mybir.dt.float32, mybir.dt.float32r, mybir.dt.bfloat16
    ALU = mybir.AluOpType
    ACT = mybir.ActivationFunctionType
    AX = mybir.AxisListType
    P = 128
    T, E = x.shape
    B = 4
    S = T // B
    QB = S // P
    HD = w0.shape[0]
    D = 64
    PAIRS = HD // P
    N = B * PAIRS
    STEPS = 2 * QB
    HALF = S // 2
    HB = QB // 2
    EXPERTS = router_t.shape[1]
    RANK = P // EXPERTS
    EPS = 1e-5
    SCALE = D ** -0.5
    MASKED = -1e30

    TURNS = [[(c, min(4, QB - k // 2 - c)) for c in range(0, QB - k // 2, 4)] for k in range(STEPS)]
    TURN0 = [sum(len(t) for t in TURNS[:k]) for k in range(STEPS)]
    NTURN = sum(len(t) for t in TURNS)
    EVACS = NTURN // 2
    EVACS0 = TURN0[STEPS // 2] // 2
    W_DMAS, STACK_DMAS, X_DMAS = 3, 6, 3
    A_LINKS, B_LINKS = 8, 21

    ctx = ExitStack()
    with ctx:
        def sb(name, shape, dt=fp32):
            return ctx.enter_context(nc.sbuf_tensor(name, shape, dt))

        def ps(name, shape, dt=fp32):
            return ctx.enter_context(nc.psum_tensor(name, shape, dt))

        def sem(name):
            return ctx.enter_context(nc.semaphore(name))

        ident = sb("ident", [P, P])
        ident_bf = sb("ident_bf", [P, P], bf16)
        mask_bf = sb("mask_bf", [P, P], bf16)
        ln_col = sb("ln_col", [P, 2])
        b0_row = sb("b0_row", [P, E])
        router_sb = sb("router_sb", [P, EXPERTS])
        down_sb = sb("down_sb", [P, P])
        up_sb = sb("up_sb", [P, E])
        up_gated = sb("up_gated", [P, E])
        minus_half = sb("minus_half", [P, QB])
        earlier = sb("earlier", [P, EXPERTS, EXPERTS])
        own = sb("own", [P, EXPERTS])
        wt = sb("wt", [P, 3, P])
        bias_col = sb("bias_col", [P, 2])
        bv_row = sb("bv_row", [P, P])
        w0_sb = sb("w0_sb", [P, E])
        w_high, w_low = (sb(f"w_{i}", [P, 2, P], fp32r) for i in ("high", "low"))
        xnt = sb("xnt", [P, S])
        x_high, x_low = (sb(f"x_{i}", [P, S], fp32r) for i in ("high", "low"))
        q_raw = sb("q_raw", [P, S])
        k_raw = sb("k_raw", [P, S])
        q_low = sb("q_low", [P, S], fp32r)
        stacks = [sb(f"stacks{i}", [P, 6, S], fp32r) for i in range(2)]
        QA, QBS, KHA, KHB, KLA, KLB = range(6)
        v_sb = [sb(f"v_sb{i}", [P, QB, P]) for i in range(2)]
        probs = [sb(f"probs{i}", [P, S]) for i in range(2)]
        turned = sb("turned", [P, 2 * QB * HALF + 2 * HB * HALF])
        turned0 = turned[:, 0:2 * QB * HALF].rearrange("p (h j q) -> p h j q", h=2, j=QB)
        turned1 = turned[:, 2 * QB * HALF:].rearrange("p (h j q) -> p h j q", h=2, j=HB)
        neg_max = sb("neg_max", [P, STEPS])
        sums = [sb(f"sums{i}", [P, 2, QB]) for i in range(2)]
        inv_sums = sb("inv_sums", [P, 2, QB])
        inv_row = sb("inv_row", [P, S])
        o_raw = sb("o_raw", [P, S])
        o_norm = sb("o_norm", [P, S])
        acc = sb("acc", [P, T // P, E])
        gate = sb("gate", [P, 8, EXPERTS])
        rank8 = sb("rank8", [P, 2, EXPERTS, EXPERTS])
        first_tok = sb("first_tok", [P, P])

        x_a = sb("x_a", [P, QB, E])
        y_a = sb("y_a", [P, QB, E])
        z_a = sb("z_a", [P, QB, E])
        zt_a = sb("zt_a", [P, S])
        x_b = sb("x_b", [P, QB, E])
        res_b = sb("res_b", [P, QB, E])
        u_b = sb("u_b", [P, QB, E])
        u_t = sb("u_t", [P, S])
        dg_t = u_t
        zt_high, zt_low = (i[:].rearrange("p t e -> p (t e)").bitcast(fp32r) for i in (x_a, y_a))
        stats = [sb(f"stats{i}", [P, QB, 6]) for i in range(5)]
        moments = [sb(f"moments{i}", [P, 7, QB]) for i in range(5)]

        sc = [ps(f"sc{i}", [P, S]) for i in range(2)]
        tp = [ps(f"tp{i}", [P, 512]) for i in range(2)]
        po = ps("po", [P, HALF])
        pp = ps("pp", [P, 512])

        s_small, s_const = sem("s_small"), sem("s_const")
        s_xa, s_xb = sem("s_xa"), sem("s_xb")
        s_da, s_db = sem("s_da"), sem("s_db")
        s_va, s_vb = sem("s_va"), sem("s_vb")
        s_pa, s_pb = sem("s_pa"), sem("s_pb")
        s_ya = sem("s_ya")
        s_dt, s_vt, s_pt = sem("s_dt"), sem("s_vt"), sem("s_pt")
        s_z0 = sem("s_z0")
        s_z = sem("s_z")
        s_zt = sem("s_zt")
        s_xnt = sem("s_xnt")
        s_zt_high = sem("s_zt_high")
        s_zt_cut = sem("s_zt_cut")
        s_x = sem("s_x")
        s_y = sem("s_y")
        s_r = sem("s_r")
        s_x1 = sem("s_x1")
        s_u = sem("s_u")
        s_ut = sem("s_ut")
        s_ut_out = sem("s_ut_out")
        s_first = sem("s_first")
        s_logit = sem("s_logit")
        s_lcopy = sem("s_lcopy")
        s_lm = sem("s_lm")
        s_ge = sem("s_ge")
        s_gate = sem("s_gate")
        s_down = sem("s_down")
        s_dg = sem("s_dg")
        s_upg = sem("s_upg")
        s_up = sem("s_up")
        s_f = sem("s_f")
        s_n3 = sem("s_n3")
        s_res = sem("s_res")
        s_out = sem("s_out")
        s_w = sem("s_w")
        s_w_high = sem("s_w_high")
        s_w_cut = sem("s_w_cut")
        s_w0 = sem("s_w0")
        s_qk = sem("s_qk")
        s_q_out = sem("s_q_out")
        s_k_out = sem("s_k_out")
        s_q_high = sem("s_q_high")
        s_k_high = sem("s_k_high")
        s_cut = sem("s_cut")
        s_q_cut = sem("s_q_cut")
        s_k_cut = sem("s_k_cut")
        s_stack = sem("s_stack")
        s_v = sem("s_v")
        s_v_out = sem("s_v_out")
        s_score = sem("s_score")
        s_max = sem("s_max")
        s_exp = sem("s_exp")
        s_turn = sem("s_turn")
        s_ta, s_td = sem("s_ta"), sem("s_td")
        s_pv0, s_pv1 = sem("s_pv0"), sem("s_pv1")
        s_o_out = sem("s_o_out")
        s_inv = sem("s_inv")
        s_inv_out = sem("s_inv_out")
        s_inv_row = sem("s_inv_row")
        s_norm = sem("s_norm")
        s_w0p = sem("s_w0p")
        s_acc = sem("s_acc")

        block = ctx.enter_context(nc.Block())

        def pairs(eng, body, period=False):
            def sided(c, after, before):
                for i in range(4):
                    body(c * PAIRS + 1 + i, (1 + i) % 2, False, False, (i, c, after, before))

            def plain(c, count):
                if period:
                    for i in range(4, 4 + 2 * count):
                        body(c * PAIRS + 1 + i, (1 + i) % 2, False, False, (i, c, False, count > 1))
                    return
                with eng.Fori(0, count) as t:
                    body(c * PAIRS + t * 2 + 5, 1, False, False, None)
                    body(c * PAIRS + t * 2 + 6, 0, False, False, None)

            body(0, 0, True, False, None)
            sided(0, False, True)
            plain(0, (PAIRS - 4) // 2)
            with eng.Fori(1, B - 1) as c:
                sided(c, True, True)
                plain(c, (PAIRS - 4) // 2)
            sided(B - 1, True, False)
            plain(B - 1, (PAIRS - 6) // 2)
            body(N - 1, 1, False, True, None)

        def reach(eng, semaphore, count):
            if not (isinstance(count, int) and count == 0):
                eng.wait_ge(semaphore, count)

        @block.sync
        def _(sp):
            def load_x(dst, c, done):
                sp.dma_start(dst[:], x[bass.ds(c * S, S), :].rearrange("(t p) e -> p t e", p=P)).then_inc(done, 16)

            def load_weights(n):
                p, column = n % PAIRS, (n % PAIRS) * P
                sp.dma_start(wt[:].rearrange("p a c -> p (a c)"),
                             w_pairs[bass.ds(p, 1), :, :].rearrange("o p n -> (o p) n")).then_inc(s_w, 16)
                sp.dma_start(bias_col[:], qk_bias[bass.ds(p, 1), :, :].rearrange("o p n -> (o p) n")).then_inc(s_w, 16)
                sp.dma_start(bv_row[:], bv[0:1, bass.ds(column, P)].to_broadcast([P, P])).then_inc(s_w, 16)

            def move_q(n, parity):
                st, q_lo = stacks[parity][:].bitcast(fp32), q_low[:].bitcast(fp32)
                sp.wait_ge(s_q_cut, n + 1)
                sp.dma_start(st[D:P, QA, :], q_lo[0:D, :]).then_inc(s_stack, 16)
                sp.dma_start(st[0:D, QBS, :], q_lo[D:P, :]).then_inc(s_stack, 16)

            def move_k(n, parity, a, b, done):
                st = stacks[parity][:].bitcast(fp32)
                sp.wait_ge(done, n + 1)
                sp.dma_start(st[D:P, a, :], st[0:D, a, :]).then_inc(s_stack, 16)
                sp.dma_start(st[0:D, b, :], st[D:P, b, :]).then_inc(s_stack, 16)

            def spread_sums(g):
                sp.wait_ge(s_inv, g + 1)
                sp.dma_start(sums_dram.rearrange("h p i -> p h i"), inv_sums[:]).then_inc(s_inv_out, 16)
                sp.wait_ge(s_inv_out, 16 * (g + 1))
                for h in range(2):
                    sp.dma_start(inv_row[h * D:(h + 1) * D, :],
                                 sums_dram[h:h + 1, :, :].rearrange("o p i -> o (p i)").to_broadcast([D, S])
                                 ).then_inc(s_inv_row, 16)

            def spread_half(half):
                sp.wait_ge(s_inv, N + half)
                dram = sums_dram[half:half + 1, :, :].rearrange("o p i -> (o p i)").rearrange("(h p i) -> h p i", h=2, p=P)
                sp.dma_start(dram.rearrange("h p i -> p h i"), inv_sums[:, :, half * HB:(half + 1) * HB]).then_inc(s_inv_out, 16)
                sp.wait_ge(s_inv_out, 16 * (N + half))
                for h in range(2):
                    sp.dma_start(inv_row[h * D:(h + 1) * D, half * HALF:(half + 1) * HALF],
                                 dram[h:h + 1, :, :].rearrange("o p i -> o (p i)").to_broadcast([D, HALF])
                                 ).then_inc(s_inv_row, 16)

            def move_x(c):
                for dst, src in ((xnt[:], zt_a[:]), (x_high[:].bitcast(fp32), zt_high.bitcast(fp32)),
                                 (x_low[:].bitcast(fp32), zt_low.bitcast(fp32))):
                    sp.dma_start(dst, src).then_inc(s_x, 16)

            def store_result(c):
                sp.wait_ge(s_res, c + 1)
                sp.dma_start(out[bass.ds(c * S, S), :].rearrange("(t p) e -> p t e", p=P), res_b[:]).then_inc(s_out, 16)

            load_x(x_a, 0, s_x)
            for dst, src in ((ln_col[:], ln_gb), (router_sb[:], router_t), (down_sb[:], down_t),
                             (up_sb[:], up_r), (b0_row[:], b0.to_broadcast([P, E]))):
                sp.dma_start(dst, src).then_inc(s_small, 16)
            load_weights(0)
            move_k(0, 0, KHA, KHB, s_k_high)
            sp.wait_ge(s_v_out, 2)
            sp.wait_ge(s_k_out, 2)
            load_weights(1)
            move_q(0, 0)
            move_k(0, 0, KLA, KLB, s_k_cut)

            def pair(g, parity, first, last, side):
                i, c, after, before = side or (None, 0, False, False)
                if i == 0 and after:
                    load_x(x_b, c - 1, s_xb)
                if i == 0 and before:
                    if not (isinstance(c, int) and c == 0):
                        sp.wait_ge(s_x, 16 * X_DMAS * c + 16)
                    load_x(x_a, c + 1, s_xa)
                if i == 5 and before:
                    sp.wait_ge(s_zt_cut, c + 2)
                if not first:
                    spread_sums(g - 1)
                if not last:
                    move_q(g + 1, 1 - parity)
                    move_k(g + 1, 1 - parity, KHA, KHB, s_k_high)
                    move_k(g + 1, 1 - parity, KLA, KLB, s_k_cut)
                    sp.wait_ge(s_v_out, 2 * g + 4)
                    sp.wait_ge(s_k_out, 2 * g + 4)
                    if i == 5 and before:
                        move_x(c + 1)
                    load_weights((g + 2) % N)
                if not first:
                    sp.wait_ge(s_acc, 2 * g)
                sp.dma_start(w0_sb[:], w0[bass.ds((g % PAIRS) * P, P), :]).then_inc(s_w0, 16)
                if i == 3 and after:
                    store_result(c - 1)

            pairs(sp, pair, period=True)
            load_x(x_b, B - 1, s_xb)
            for half in range(2):
                spread_half(half)
            for half in range(2):
                sp.wait_ge(s_res, B + half)
                sp.dma_start(out[(B - 1) * S + half * HALF:(B - 1) * S + (half + 1) * HALF, :]
                             .rearrange("(t p) e -> p t e", p=P), res_b[:, half * HB:(half + 1) * HB, :]).then_inc(s_out, 16)
            sp.wait_ge(s_out, 16 * (B + 1))
            sp.wait_ge(s_w, 16 * W_DMAS * (N + 1))

        @block.gpsimd
        def _(pool):
            nc.gpsimd.memset(minus_half[:], -0.5)
            nc.gpsimd.memset(ident[:], 0.0)
            nc.gpsimd.memset(ident_bf[:], 0.0)
            nc.gpsimd.memset(mask_bf[:], 0.0)
            nc.gpsimd.memset(earlier[:], 1.0)
            nc.gpsimd.memset(own[:], 1.0).then_inc(s_const, 1)
            pool.wait_ge(s_const, 1)
            nc.gpsimd.affine_select(out=ident[:], in_=ident[:], compare_op=ALU.not_equal, fill=1.0, base=0,
                                    pattern=[[-1, P]], channel_multiplier=1)
            nc.gpsimd.affine_select(out=ident_bf[:], in_=ident_bf[:], compare_op=ALU.not_equal, fill=1.0, base=0,
                                    pattern=[[-1, P]], channel_multiplier=1)
            nc.gpsimd.affine_select(out=mask_bf[:], in_=mask_bf[:], compare_op=ALU.is_ge, fill=MASKED, base=0,
                                    pattern=[[1, P]], channel_multiplier=-1)
            nc.gpsimd.affine_select(out=earlier[:], in_=earlier[:], compare_op=ALU.is_ge, fill=0.0, base=-1,
                                    pattern=[[1, EXPERTS], [-1, EXPERTS]], channel_multiplier=0)
            nc.gpsimd.affine_select(out=own[:], in_=own[:], compare_op=ALU.is_ge, fill=0.0, base=0,
                                    pattern=[[-RANK, EXPERTS]], channel_multiplier=1).then_inc(s_const, 1)
            pool.wait_ge(s_const, 2)
            nc.gpsimd.affine_select(out=own[:], in_=own[:], compare_op=ALU.is_ge, fill=0.0, base=RANK - 1,
                                    pattern=[[RANK, EXPERTS]], channel_multiplier=-1).then_inc(s_const, 1)

            def inverse_roots(norm, c):
                made, done, count = (s_va, s_pa, (c - 1) * 2 + 1 + norm) if norm < 2 else (s_vb, s_pb, c * 3 + norm - 1)
                pool.wait_ge(made, count)
                m = moments[norm]
                nc.gpsimd.tensor_tensor(m[:, 6, :], m[:, 5, :], minus_half[:], ALU.pow).then_inc(done, 1)
                pool.wait_ge(done, count)

            def inverse_roots_of(norm, part, count):
                pool.wait_ge(s_vt, count)
                m = moments[norm]
                nc.gpsimd.tensor_tensor(m[:, 6, part], m[:, 5, part], minus_half[:, part], ALU.pow).then_inc(s_pt, 1)
                pool.wait_ge(s_pt, count)

            def start_acc(c):
                pool.wait_ge(s_ya, c + 1)
                nc.gpsimd.tensor_tensor(acc[:, bass.ds(c * QB, QB), :], y_a[:],
                                        b0_row[:].unsqueeze(1).to_broadcast([P, QB, E]), ALU.add).then_inc(s_y, 1)
                pool.wait_ge(s_y, c + 1)

            def add_x(c):
                pool.wait_ge(s_xb, 16 * (c + 1))
                pool.wait_ge(s_r, c + 1)
                nc.gpsimd.tensor_tensor(x_b[:], x_b[:], res_b[:], ALU.add).then_inc(s_x1, 1)
                pool.wait_ge(s_x1, c + 1)

            h0, h1 = slice(0, HB), slice(HB, QB)
            for count, (norm, part) in enumerate(((0, h0), (0, h1), (1, h0), (1, h1))):
                inverse_roots_of(norm, part, count + 1)
            pool.wait_ge(s_small, 16 * 5)
            start_acc(0)

            def low(dst, src, hi):
                return nc.gpsimd.tensor_tensor(dst, src, hi.bitcast(fp32), ALU.subtract)

            def cut_q(n, parity):
                st = stacks[parity]
                pool.wait_ge(s_q_high, n + 1)
                if isinstance(n, int) and n == 1:
                    pool.wait_ge(s_w_cut, 1)
                else:
                    pool.wait_ge(s_norm, 2 * n - 3)
                pool.wait_ge(s_stack, 16 * STACK_DMAS * n)
                low(q_low[0:D, :], q_raw[0:D, :], st[0:D, QA, :]).then_inc(s_cut, 1)
                pool.wait_ge(s_cut, 2 * n + 1)
                low(q_low[D:P, :], q_raw[D:P, :], st[D:P, QBS, :]).then_inc(s_q_cut, 1)

            def cut_k(n, parity):
                st = stacks[parity]
                if isinstance(n, int) and n == 0:
                    pool.wait_ge(s_y, 1)
                elif isinstance(n, int) and n == 1:
                    pool.wait_ge(s_q_cut, 2)
                else:
                    reach(pool, s_norm, 2 * (n - 1))
                pool.wait_ge(s_k_high, n + 1)
                low(st[0:D, KLA, :], k_raw[0:D, :], st[0:D, KHA, :]).then_inc(s_cut, 1)
                pool.wait_ge(s_cut, 2 * n + 2)
                low(st[D:P, KLB, :], k_raw[D:P, :], st[D:P, KHB, :]).then_inc(s_k_cut, 1)

            def cut_zt(c):
                pool.wait_ge(s_zt_high, c + 1)
                low(zt_low, zt_a[:], zt_high).then_inc(s_zt_cut, 1)
                pool.wait_ge(s_zt_cut, c + 1)

            def cut_w(n):
                pool.wait_ge(s_w_high, n)
                low(w_low[:], wt[:, 0:2, :], w_high[:]).then_inc(s_w_cut, 1)

            def normalise(g, half, before, count):
                apart = isinstance(g, int) and g == N - 1
                if apart:
                    inv = inv_row[:, half * HALF:(half + 1) * HALF].rearrange("p (q i) -> p i q", i=HB)
                else:
                    inv = inv_row[:].rearrange("p (q i) -> p i q", i=QB)[:, half * HB:(half + 1) * HB, :]
                pool.wait_ge(before, count)
                if half == 0 or apart:
                    pool.wait_ge(s_inv_row, 32 * (g + 1 + half * apart))
                reach(pool, s_w0p, 2 * g)
                pool.wait_ge(s_o_out, 2 * g + 1 + half)
                q = slice(half * HALF, (half + 1) * HALF)
                nc.gpsimd.tensor_tensor(o_norm[:, q].rearrange("p (i q) -> p i q", q=P),
                                        o_raw[:, q].rearrange("p (i q) -> p i q", q=P),
                                        inv, ALU.mult).then_inc(s_norm, 1)

            cut_k(0, 0)
            pool.wait_ge(s_k_cut, 1)
            cut_w(1)

            def pair(g, parity, first, last, side):
                i, c, after, before = side or (None, 0, False, False)
                if (i == 1 and after) or (i == 2 and before):
                    pool.wait_ge(s_w_cut, g + 1)
                    if i == 1:
                        add_x(c - 1)
                    else:
                        start_acc(c + 1)
                if not first:
                    normalise(g - 1, 0, s_w_cut, N if last else g + 1)
                if not last:
                    cut_q(g + 1, 1 - parity)
                if not first:
                    normalise(g - 1, 1, *((s_norm, 2 * g - 1) if last else (s_q_cut, g + 2)))
                if i == 3 and after:
                    pool.wait_ge(s_norm, 2 * g)
                    inverse_roots(4, c - 1)
                if not last:
                    cut_k(g + 1, 1 - parity)
                roots = {0: [(2, c - 1)] * after + [(0, c + 1)] * before, 1: [(3, c - 1)] * after,
                         2: [(1, c + 1)] * before}.get(i)
                if not last:
                    pool.wait_ge(s_k_cut, g + 2)
                    for root in roots or ():
                        inverse_roots(*root)
                    if i == 3 and before:
                        cut_zt(c + 1)
                    cut_w(g + 2)

            pairs(pool, pair)
            normalise(N - 1, 0, s_norm, 2 * N - 2)
            pool.wait_ge(s_norm, 2 * N - 1)
            inverse_roots_of(2, h0, 5)
            normalise(N - 1, 1, s_norm, 2 * N - 1)
            pool.wait_ge(s_norm, 2 * N)
            for count, (norm, part) in enumerate(((3, h0), (2, h1), (3, h1), (4, h0), (4, h1))):
                inverse_roots_of(norm, part, count + 6)

        @block.tensor
        def _(pe):
            def turn_four(src, a, bank=pp):
                for j in range(4):
                    last = nc.tensor.transpose(bank[:, j * P:(j + 1) * P], src[:, 4 * a + j, :], ident[:])
                return last

            def turn_z(c, a, bank=pp, done=None):
                pe.wait_ge(done or s_z, c + 1)
                turn_four(z_a, a, bank).then_inc(s_zt, 1)
                return s_xnt, c * 2 + a + 1

            def turn_u(c, a, bank=pp, later=0):
                pe.wait_ge(s_u, c + 1 + later)
                turn_four(u_b, a, bank).then_inc(s_ut, 1)
                return s_ut_out, c * 2 + a + 1

            def logits(c, bank=pp):
                pe.wait_ge(s_first, c + 1)
                nc.tensor.matmul(bank[:, 0:EXPERTS], first_tok[:], router_sb[:], start=True, stop=True).then_inc(s_logit, 1)
                return s_lcopy, c + 1

            def project_down(c, a, bank=pp):
                pe.wait_ge(s_ut_out, c * 2 + a + 1)
                nc.tensor.matmul(bank[:, 0:512], down_sb[:], u_t[:, a * 512:(a + 1) * 512], start=True,
                                 stop=True).then_inc(s_down, 1)
                return s_dg, c * 2 + a + 1

            def project_up(c, a, bank=pp):
                pe.wait_ge(s_dg, c * 2 + a + 1)
                pe.wait_ge(s_upg, c + 1)
                for j in range(4):
                    t = 4 * a + j
                    last = nc.tensor.matmul(bank[:, j * P:(j + 1) * P], dg_t[:, t * P:(t + 1) * P], up_gated[:],
                                            start=True, stop=True)
                last.then_inc(s_up, 1)
                return s_f, c * 2 + a + 1

            pe.wait_ge(s_const, 3)
            pe.wait_ge(s_small, 16 * 5)
            turn_z(0, 0, tp[0], s_z0)
            turn_z(0, 1, tp[1])

            def project_first(part, bank):
                c = part % 2
                nc.tensor.matmul(bank[:], wt[:, part // 2, :], xnt[:, c * HALF:(c + 1) * HALF],
                                 start=True, stop=True).then_inc(s_qk, 1)

            def project(n, part):
                if part == 0:
                    pe.wait_ge(s_w_cut, n)
                    pe.wait_ge(s_x, 16 * X_DMAS * (n // PAIRS) + 16)
                w, c = part // 2, part % 2
                tokens = slice(c * HALF, (c + 1) * HALF)
                nc.tensor.matmul(pp[:], w_high[:, w, :], x_low[:, tokens], start=True, stop=False)
                nc.tensor.matmul(pp[:], w_low[:, w, :], x_high[:, tokens], start=False, stop=False)
                nc.tensor.matmul(pp[:], w_high[:, w, :], x_high[:, tokens], start=False,
                                 stop=True).then_inc(s_qk, 1)

            def project_v(n, c, bank=pp):
                for j in range(4):
                    t = 4 * c + j
                    last = nc.tensor.matmul(bank[:, j * P:(j + 1) * P], xnt[:, t * P:(t + 1) * P], wt[:, 2, :],
                                            start=True, stop=True)
                last.then_inc(s_v, 1)

            def scores(g, parity, k):
                i, h = k // 2, k % 2
                st = stacks[parity]
                width = (QB - i) * P
                for o in reversed(range(0, width, 512)):
                    w = min(512, width - o)
                    dst = sc[k % 2][:, o:o + w]
                    q = st[:, QA + h, i * P:(i + 1) * P]
                    keys = slice(i * P + o, i * P + o + w)
                    nc.tensor.matmul(dst, q, st[:, KHA + h, keys], start=True, stop=False)
                    last = nc.tensor.matmul(dst, q, st[:, KLA + h, keys], start=False, stop=(o > 0))
                    if o == 0:
                        last = nc.tensor.matmul(dst[:, 0:P], ident_bf[:], mask_bf[:], start=False, stop=True)
                last.then_inc(s_score, 1)

            def turn(g, k):
                pe.wait_ge(s_exp, STEPS * g + k + 1)
                for n, (c0, m) in enumerate(TURNS[k]):
                    t = TURN0[k] + n
                    if t >= 2 or not (isinstance(g, int) and g == 0):
                        pe.wait_ge((s_td, s_ta)[t % 2], EVACS * g + t // 2)
                    for j in range(m):
                        last = nc.tensor.transpose(tp[t % 2][:, j * P:(j + 1) * P],
                                                   probs[k % 2][:, (c0 + j) * P:(c0 + j + 1) * P], ident[:])
                    last.then_inc(s_turn, 1)

            def outputs(g, parity, half, blocks):
                for j in blocks:
                    w = min(HB, j + 1 - half * HB) * P
                    for h in range(2):
                        src = (turned0 if half == 0 else turned1)[:, h, j - half * HB, 0:w]
                        last = nc.tensor.matmul(po[h * D:(h + 1) * D, 0:w], v_sb[parity][:, j, h * D:(h + 1) * D],
                                                src, start=(j == QB - 1), stop=(j == half * HB))
                if j == half * HB:
                    last.then_inc((s_pv0, s_pv1)[half], 1)

            def project_out(g, c, bank=pp):
                pe.wait_ge(s_norm, 2 * g + 1 + c)
                if c == 0:
                    pe.wait_ge(s_w0, 16 * (g + 1))
                for j in range(4):
                    t = 4 * c + j
                    last = nc.tensor.matmul(bank[:, j * P:(j + 1) * P], o_norm[:, t * P:(t + 1) * P], w0_sb[:],
                                            start=True, stop=True)
                last.then_inc(s_w0p, 1)

            pe.wait_ge(s_w, 16 * W_DMAS)
            pe.wait_ge(s_xnt, 1)
            project_first(0, pp)
            project_first(2, po)
            pe.wait_ge(s_xnt, 2)
            project_first(1, tp[0])
            project_first(3, tp[1])
            project_v(0, 0, sc[1][:, 0:512])
            project_v(0, 1, sc[1][:, 512:1024])

            AFTER = {1: {14: (turn_u, 0), 15: (turn_u, 1)},
                     2: {10: (logits,), 11: (project_down, 0), 12: (project_down, 1),
                         14: (project_up, 0), 15: (project_up, 1)}}
            BEFORE = {3: {11: (turn_z, 0), 12: (turn_z, 1)}}

            def pair(g, parity, first, last, side):
                n = g + 1
                i, c, after, before = side or (None, 0, False, False)
                busy = []

                def pp_after(semaphore, count):
                    reach(pe, semaphore, count)

                for k in range(STEPS):
                    if k == 0:
                        pe.wait_ge(s_stack, 16 * STACK_DMAS * (g + 1))
                    if k > 1 or not first:
                        pe.wait_ge(s_exp, STEPS * g + k - 1)
                    scores(g, parity, k)
                    if k == 0 and not first:
                        turn(g - 1, STEPS - 1)
                    if k == 0 and not last:
                        if after and i > 1:
                            pp_after(s_ut_out if i == 2 else s_f, 2 * c)
                        else:
                            pp_after(*((s_v_out, 2) if first else (s_acc, 2 * (g - 1))))
                        project(n, 0)
                    if k == 1 and not first:
                        pe.wait_ge(s_ta, EVACS * g)
                        pe.wait_ge(s_td, EVACS * g)
                        pe.wait_ge(s_o_out, 2 * g - 1)
                        outputs(g - 1, 1 - parity, 1, (7,))
                    if k == 2 and not last:
                        pp_after(s_q_out, 2 * n + 1)
                        project(n, 1)
                    if k == 3 and not last:
                        pp_after(s_q_out, 2 * n + 2)
                        project(n, 2)
                    if k == 4 and not first:
                        pp_after(*((s_acc, 2 * (g - 1)) if last else (s_k_out, 2 * n + 1)))
                        project_out(g - 1, 0)
                    if k == 5 and not last:
                        pp_after(*((s_k_out, 2 * n + 1) if first else (s_acc, 2 * g - 1)))
                        project(n, 3)
                    if k in (3, 6) and not first:
                        outputs(g - 1, 1 - parity, 1, {3: (6,), 6: (5, 4)}[k])
                    if k == 7 and not last:
                        pp_after(s_k_out, 2 * n + 2)
                        project_v(n, 0)
                    if k == 8 and not last:
                        pp_after(s_v_out, 2 * n + 1)
                        project_v(n, 1)
                    if k == 9 and not first:
                        pp_after(*((s_acc, 2 * g - 1) if last else (s_v_out, 2 * n + 2)))
                        project_out(g - 1, 1)
                    if k == (9 if last else 10):
                        pe.wait_ge(s_ta, EVACS * g + EVACS0)
                        pe.wait_ge(s_td, EVACS * g + EVACS0)
                        if not first:
                            pe.wait_ge(s_o_out, 2 * g)
                    blocks = ({9: (7,), 10: (6, 5), 11: (4, 3, 2, 1, 0)} if last else
                              {10: (7,), 11: (6,), 12: (5,), 13: (4,), 14: (3, 2), 15: (1, 0)}).get(k)
                    if blocks:
                        outputs(g, parity, 0, blocks)
                    if k == 15 and last:
                        pp_after(s_acc, 2 * g)
                        project_out(g, 0)
                    for wanted, table, b in ((after, AFTER, c - 1), (before, BEFORE, c + 1)):
                        if wanted and k in table.get(i, {}):
                            use, *part = table[i][k]
                            pp_after(*(busy.pop() if busy else (s_acc, 2 * g)))
                            busy.append(use(b, *part))
                    if k:
                        turn(g, k - 1)
            pairs(pe, pair)
            g = N - 1
            turn(g, STEPS - 1)
            pe.wait_ge(s_ta, EVACS * N)
            pe.wait_ge(s_td, EVACS * N)
            pe.wait_ge(s_o_out, 2 * g + 1)
            outputs(g, 1, 1, (7, 6, 5, 4))
            pe.wait_ge(s_ta, EVACS * N)
            project_out(g, 1, tp[0])
            b = B - 1
            turn_u(b, 0, sc[0][:, 0:512])
            logits(b, tp[1])
            project_down(b, 0, sc[1][:, 0:512])
            turn_u(b, 1, sc[0][:, 512:1024], 1)
            project_up(b, 0)
            project_down(b, 1, sc[1][:, 512:1024])
            project_up(b, 1, tp[0])

        @block.scalar
        def _(act):
            act.wait_ge(s_const, 3)
            nc.scalar.activation(inv_sums[:, 0, 0:1], ident[:, 0:1], ACT.Exp)
            act.wait_ge(s_small, 16 * 5)

            def take_z(c, a, dst, bank=pp):
                act.wait_ge(s_zt, c * 2 + a + 1)
                nc.scalar.activation(dst[:, a * 512:(a + 1) * 512], bank[:], ACT.Identity,
                                     bias=ln_col[:, 1:2], scale=ln_col[:, 0:1]).then_inc(s_xnt, 1)

            def take_u(c, a, bank=pp):
                act.wait_ge(s_ut, c * 2 + a + 1)
                nc.scalar.copy(u_t[:, a * 512:(a + 1) * 512], bank[:, 0:512]).then_inc(s_ut_out, 1)

            def spread_first(c):
                act.wait_ge(s_ut_out, c * 2 + 1)
                nc.scalar.copy(first_tok[:], u_t[:, 0:1].to_broadcast([P, P])).then_inc(s_first, 1)

            def exp_logits(c):
                act.wait_ge(s_lm, c + 1)
                nc.scalar.activation(gate[:, 2, :], gate[:, 0, :], ACT.Exp, bias=gate[:, 1, 0:1]).then_inc(s_ge, 1)

            def take_down(c, a, bank=pp):
                act.wait_ge(s_down, c * 2 + a + 1)
                nc.scalar.copy(dg_t[:, a * 512:(a + 1) * 512], bank[:, 0:512]).then_inc(s_dg, 1)

            def gate_up(c):
                act.wait_ge(s_gate, c + 1)
                nc.scalar.activation(up_gated[:], up_sb[:], ACT.Copy, scale=gate[:, 7, 0:1]).then_inc(s_upg, 1)

            take_z(0, 0, xnt, tp[0])
            take_z(0, 1, xnt, tp[1])

            def take_k(n, c, wait, bank=pp):
                act.wait_ge(s_qk, 4 * n + (3 + c if wait else 2 + 2 * c))
                if wait:
                    act.wait_ge(s_k_cut, n)
                nc.scalar.activation(k_raw[:, c * HALF:(c + 1) * HALF], bank[:], ACT.Identity,
                                     bias=bias_col[:, 1:2]).then_inc(s_k_out, 1)

            def take_o(g, half):
                act.wait_ge((s_pv0, s_pv1)[half], g + 1)
                if not (isinstance(g, int) and g == 0):
                    act.wait_ge(s_norm, 2 * (g - 1) + 1 + half)
                nc.scalar.copy(o_raw[:, half * HALF:(half + 1) * HALF], po[:]).then_inc(s_o_out, 1)

            def take_turn(g, k):
                i, h = k // 2, k % 2
                for n, (c0, m) in enumerate(TURNS[k]):
                    t = TURN0[k] + n
                    if t % 2 == 0:
                        continue
                    reach(act, s_pv0 if i < HB else s_pv1, g)
                    act.wait_ge(s_turn, NTURN * g + t + 1)
                    dst, at = (turned0, 0) if i < HB else (turned1, HB)
                    nc.scalar.copy(dst[:, h, i + c0 - at:i + c0 - at + m, (i - at) * P:(i - at + 1) * P],
                                   tp[1][:, 0:m * P].rearrange("p (j q) -> p j q", q=P)).then_inc(s_ta, 1)

            act.wait_ge(s_w, 16 * W_DMAS)
            take_k(0, 0, False, po)
            take_k(0, 1, False, tp[1])

            AFTER = {1: {14: lambda b: (take_u(b, 0), spread_first(b)), 15: lambda b: take_u(b, 1)},
                     2: {11: lambda b: (exp_logits(b), take_down(b, 0)), 12: lambda b: take_down(b, 1), 13: gate_up}}
            BEFORE = {3: {11: lambda b: take_z(b, 0, zt_a), 12: lambda b: take_z(b, 1, zt_a)}}

            def pair(g, parity, first, last, side):
                stage, c, after, before = side or (None, 0, False, False)
                for k in range(STEPS):
                    i, h = k // 2, k % 2
                    width = (QB - i) * P
                    if k == 3 and not last:
                        take_k(g + 1, 0, True)
                    if k == 5 and not last:
                        take_k(g + 1, 1, True)
                    if k == 0 and not first:
                        take_turn(g - 1, STEPS - 1)
                    act.wait_ge(s_max, STEPS * g + k + 1)
                    if k == 0 and not first:
                        act.wait_ge(s_inv, g)
                    nc.scalar.activation(probs[k % 2][:, 0:width], sc[k % 2][:, 0:width], ACT.Exp,
                                         bias=neg_max[:, k:k + 1],
                                         accum_out=sums[parity][:, h, i:i + 1]).then_inc(s_exp, 1)
                    if k == 6 and not first:
                        take_o(g - 1, 1)
                    if k == (12 if last else 15):
                        take_o(g, 0)
                    if k:
                        take_turn(g, k - 1)
                    for wanted, table, b in ((after, AFTER, c - 1), (before, BEFORE, c + 1)):
                        if wanted and k in table.get(stage, {}):
                            table[stage][k](b)

            pairs(act, pair)
            take_turn(N - 1, STEPS - 1)
            take_o(N - 1, 1)

            b = B - 1
            take_u(b, 0, sc[0][:, 0:512])
            spread_first(b)
            exp_logits(b)
            take_down(b, 0, sc[1][:, 0:512])
            gate_up(b)
            take_u(b, 1, sc[0][:, 512:1024])
            take_down(b, 1, sc[1][:, 512:1024])

        @block.vector
        def _(dve):
            links = {s_da: 0, s_db: 0, s_dt: 0}

            def link(ins, semaphore, c):
                if semaphore is s_dt:
                    links[s_dt] += 1
                    ins.then_inc(s_dt, 1)
                    return dve.wait_ge(s_dt, links[s_dt])
                per_batch = A_LINKS if semaphore is s_da else B_LINKS
                links[semaphore] = links[semaphore] % per_batch + 1
                ins.then_inc(semaphore, 1)
                before = (c - 1 if semaphore is s_da else c) * per_batch
                dve.wait_ge(semaphore, before + links[semaphore])

            def chain_of(norm):
                return s_da if norm < 2 else s_db

            def norm_stats(norm, src, c, blocks):
                for t in blocks:
                    last = nc.vector.bn_stats(stats[norm][:, t, :], src[:, t, :])
                if QB - 1 in blocks:
                    link(last, chain_of(norm), c)

            def norm_moments(norm, c, part=slice(0, QB), by=None):
                m, by = moments[norm], by or chain_of(norm)
                me, qe, mo, qo = (stats[norm][:, part, a:a + 1].rearrange("p t o -> p (t o)") for a in (1, 2, 4, 5))
                nc.vector.tensor_tensor(m[:, 0, part], me, mo, ALU.add)
                nc.vector.tensor_tensor(m[:, 1, part], me, mo, ALU.subtract)
                link(nc.vector.tensor_tensor(m[:, 2, part], qe, qo, ALU.add), by, c)
                nc.vector.tensor_scalar(m[:, 3, part], m[:, 0, part], 0.5, None, ALU.mult)
                link(nc.vector.tensor_tensor(m[:, 4, part], m[:, 1, part], m[:, 1, part], ALU.mult), by, c)
                link(nc.vector.scalar_tensor_tensor(out=m[:, 4, part], in0=m[:, 4, part], scalar=E / 4,
                                                    in1=m[:, 2, part], op0=ALU.mult, op1=ALU.add), by, c)
                nc.vector.tensor_scalar(m[:, 5, part], m[:, 4, part], 1.0 / E, EPS, ALU.mult,
                                        ALU.add).then_inc(s_vt if by is s_dt else s_va if norm < 2 else s_vb, 1)

            def norm_apply(norm, dst, src, c, blocks, done):
                if 0 in blocks:
                    dve.wait_ge(*((s_pa, (c - 1) * 2 + 1 + norm) if norm < 2 else (s_pb, c * 3 + norm - 1)))
                m = moments[norm]
                for t in blocks:
                    last = nc.vector.tensor_scalar(dst[:, t, :], src[:, t, :], m[:, 3, t:t + 1], m[:, 6, t:t + 1],
                                                   ALU.subtract, ALU.mult)
                if QB - 1 in blocks:
                    last.then_inc(done, 1)

            def acc_of(c):
                return acc[:, bass.ds(c * QB, QB), :]

            def a1_stats(c, blocks):
                if 0 in blocks:
                    dve.wait_ge(s_xa, 16 * c)
                norm_stats(0, x_a, c, blocks)

            def a2_stats(c, blocks):
                if 0 in blocks:
                    dve.wait_ge(s_ya, c + 1)
                norm_stats(1, y_a, c, blocks)

            def b2_stats(c, blocks):
                if 0 in blocks:
                    dve.wait_ge(s_x1, c + 1)
                norm_stats(3, x_b, c, blocks)

            def b3_stats(c, blocks):
                if 0 in blocks:
                    dve.wait_ge(s_f, c * 2 + 2)
                norm_stats(4, u_b, c, blocks)

            def add_x1(c, blocks):
                if 0 in blocks:
                    dve.wait_ge(s_n3, c + 1)
                part = slice(blocks.start, blocks.stop)
                last = nc.vector.tensor_tensor(res_b[:, part, :], res_b[:, part, :], x_b[:, part, :], ALU.add)
                if QB - 1 in blocks:
                    last.then_inc(s_res, 1)

            def take_logits(c, bank=pp):
                dve.wait_ge(s_logit, c + 1)
                nc.vector.tensor_copy(gate[:, 0, :], bank[:, 0:EXPERTS]).then_inc(s_lcopy, 1)
                dve.wait_ge(s_lcopy, c + 1)
                nc.vector.tensor_reduce(gate[:, 1, 0:1], gate[:, 0, :], AX.X, ALU.max, negate=True).then_inc(s_lm, 1)

            def rank_logits(c):
                mine = gate[:, 0, :].unsqueeze(2).to_broadcast([P, EXPERTS, EXPERTS])
                others = gate[:, 0, :].unsqueeze(1).to_broadcast([P, EXPERTS, EXPERTS])
                nc.vector.tensor_tensor(rank8[:, 1], others, mine, ALU.is_gt)
                link(nc.vector.tensor_tensor(rank8[:, 0], others, mine, ALU.is_equal), s_db, c)
                link(nc.vector.tensor_tensor(rank8[:, 0], rank8[:, 0], earlier[:], ALU.mult), s_db, c)
                link(nc.vector.tensor_tensor(rank8[:, 0], rank8[:, 0], rank8[:, 1], ALU.add), s_db, c)
                link(nc.vector.tensor_reduce(gate[:, 3, :], rank8[:, 0], AX.X, ALU.add), s_db, c)
                link(nc.vector.tensor_scalar(gate[:, 3, :], gate[:, 3, :], 2.0, None, ALU.is_lt), s_db, c)

            def make_gate(c):
                dve.wait_ge(s_ge, c + 1)
                link(nc.vector.tensor_tensor(gate[:, 4, :], gate[:, 2, :], gate[:, 3, :], ALU.mult), s_db, c)
                link(nc.vector.tensor_tensor(gate[:, 5, :], gate[:, 4, :], own[:], ALU.mult), s_db, c)
                nc.vector.tensor_reduce(gate[:, 6, 1:2], gate[:, 5, :], AX.X, ALU.add)
                link(nc.vector.tensor_reduce(gate[:, 6, 0:1], gate[:, 4, :], AX.X, ALU.add), s_db, c)
                link(nc.vector.reciprocal(gate[:, 6, 2:3], gate[:, 6, 0:1]), s_db, c)
                nc.vector.tensor_tensor(gate[:, 7, 0:1], gate[:, 6, 1:2], gate[:, 6, 2:3],
                                        ALU.mult).then_inc(s_gate, 1)

            def take_up(c, a, bank=pp):
                dve.wait_ge(s_up, c * 2 + a + 1)
                f = u_b[:, 4 * a:4 * a + 4, :]
                nc.vector.tensor_tensor(f, bank[:].rearrange("p (j e) -> p j e", e=E), f, ALU.add).then_inc(s_f, 1)

            def spread(use, counts):
                assert sum(counts.values()) == QB
                table, t = {}, 0
                for k, m in counts.items():
                    table[k] = [lambda b, blocks=range(t, t + m): use(b, blocks)]
                    t += m
                return table

            def at(k, use):
                return {k: [use]}

            def stage_of(*tables):
                return {k: [use for t in tables for use in t.get(k, [])] for k in range(STEPS)}

            B1, B2, B3 = (lambda b: norm_moments(2, b)), (lambda b: norm_moments(3, b)), (lambda b: norm_moments(4, b))
            AFTER = {0: stage_of(spread(lambda b, t: norm_stats(2, acc_of(b), b, t), {k: 1 for k in range(8)}), at(9, B1),
                                 spread(lambda b, t: norm_apply(2, res_b, acc_of(b), b, t, s_r), {12: 2, 13: 2, 14: 2, 15: 2})),
                     1: stage_of(spread(b2_stats, {k: 1 for k in range(2, 10)}), at(10, B2),
                                 spread(lambda b, t: norm_apply(3, u_b, x_b, b, t, s_u), {12: 4, 13: 4})),
                     2: stage_of(at(10, take_logits), at(11, rank_logits), at(12, make_gate),
                                 at(14, lambda b: take_up(b, 0)), at(15, lambda b: take_up(b, 1))),
                     3: stage_of(spread(b3_stats, {0: 1, 1: 1, 2: 1, 3: 1, 4: 2, 5: 2}), at(6, B3),
                                 spread(lambda b, t: norm_apply(4, res_b, u_b, b, t, s_n3), {11: 4, 12: 4}),
                                 spread(add_x1, {13: 4, 14: 4}))}
            BEFORE = {0: stage_of(spread(a1_stats, {9: 3, 10: 3, 11: 2}), at(13, lambda b: norm_moments(0, b))),
                      1: stage_of(spread(lambda b, t: norm_apply(0, y_a, x_a, b, t, s_ya), {14: 4, 15: 4})),
                      2: stage_of(spread(a2_stats, {k: 1 for k in range(8)}), at(8, lambda b: norm_moments(1, b))),
                      3: stage_of(spread(lambda b, t: norm_apply(1, z_a, y_a, b, t, s_z), {7: 2, 8: 2, 9: 2, 10: 2}),
                                  at(13, lambda b: high_zt(b, zt_high, zt_a)))}

            def stats_of(norm, src, half):
                for t in range(half * HB, (half + 1) * HB):
                    last = nc.vector.bn_stats(stats[norm][:, t, :], src[:, t, :])
                link(last, s_dt, 0)
                norm_moments(norm, 0, slice(half * HB, (half + 1) * HB), s_dt)

            def apply_to(norm, dst, src, half, count):
                dve.wait_ge(s_pt, count)
                m = moments[norm]
                for t in range(half * HB, (half + 1) * HB):
                    last = nc.vector.tensor_scalar(dst[:, t, :], src[:, t, :], m[:, 3, t:t + 1], m[:, 6, t:t + 1],
                                                   ALU.subtract, ALU.mult)
                return last

            def high_zt(c, dst, src):
                dve.wait_ge(s_xnt, 2 * c + 2)
                nc.vector.tensor_copy(dst, src[:]).then_inc(s_zt_high, 1)

            def high_w(n):
                dve.wait_ge(s_w, 16 * W_DMAS * (n + 1))
                nc.vector.tensor_copy(w_high[:], wt[:, 0:2, :]).then_inc(s_w_high, 1)

            dve.wait_ge(s_const, 3)
            dve.wait_ge(s_x, 16)
            stats_of(0, x_a, 0)
            stats_of(0, x_a, 1)
            link(apply_to(0, y_a, x_a, 0, 1), s_dt, 0)
            stats_of(1, y_a, 0)
            last = apply_to(0, y_a, x_a, 1, 2)
            last.then_inc(s_ya, 1)
            dve.wait_ge(s_ya, 1)
            stats_of(1, y_a, 1)
            apply_to(1, z_a, y_a, 0, 3).then_inc(s_z0, 1)
            apply_to(1, z_a, y_a, 1, 4).then_inc(s_z, 1)

            def take_q(n, c, wait, bank=pp):
                dve.wait_ge(s_qk, 4 * n + (1 + c if wait else 1 + 2 * c))
                if wait:
                    dve.wait_ge(s_q_cut, n)
                nc.vector.tensor_scalar(q_raw[:, c * HALF:(c + 1) * HALF], bank[:], bias_col[:, 0:1], SCALE,
                                        ALU.add, ALU.mult).then_inc(s_q_out, 1)

            def high(n, parity, raw, a, b, out, done, c):
                dve.wait_ge(out, 2 * n + 1 + c)
                q = slice(c * HALF, (c + 1) * HALF)
                nc.vector.tensor_copy(stacks[parity][0:D, a, q], raw[0:D, q])
                last = nc.vector.tensor_copy(stacks[parity][D:P, b, q], raw[D:P, q])
                if c:
                    last.then_inc(done, 1)

            def high_q(n, parity, c):
                high(n, parity, q_raw, QA, QBS, s_q_out, s_q_high, c)

            def high_k(n, parity, c):
                high(n, parity, k_raw, KHA, KHB, s_k_out, s_k_high, c)

            def take_v(n, parity, c, wait, bank):
                dve.wait_ge(s_v, 2 * n + 1 + c)
                if wait:
                    reach(dve, s_pv1, n - 1)
                nc.vector.tensor_tensor(v_sb[parity][:, 4 * c:4 * c + 4, :],
                                        bank.rearrange("p (j d) -> p j d", d=P),
                                        bv_row[:].unsqueeze(1).to_broadcast([P, 4, P]), ALU.add).then_inc(s_v_out, 1)

            def take_turn(g, k):
                i, h = k // 2, k % 2
                for n, (c0, m) in enumerate(TURNS[k]):
                    t = TURN0[k] + n
                    if t % 2:
                        continue
                    reach(dve, s_pv0 if i < HB else s_pv1, g)
                    dve.wait_ge(s_turn, NTURN * g + t + 1)
                    dst, at = (turned0, 0) if i < HB else (turned1, HB)
                    nc.vector.tensor_copy(dst[:, h, i + c0 - at:i + c0 - at + m, (i - at) * P:(i - at + 1) * P],
                                          tp[0][:, 0:m * P].rearrange("p (j q) -> p j q", q=P)).then_inc(s_td, 1)

            def invert_sums(g, parity):
                dve.wait_ge(s_exp, STEPS * (g + 1))
                reach(dve, s_inv_out, 16 * g)
                reach(dve, s_norm, 2 * g)
                nc.vector.reciprocal(inv_sums[:], sums[parity][:]).then_inc(s_inv, 1)

            def invert_half(half):
                dve.wait_ge(s_exp, STEPS * (N - 1) + (half + 1) * (STEPS // 2))
                dve.wait_ge(s_inv_out, 16 * (N - 1 + half))
                dve.wait_ge(s_norm, 2 * N - 2)
                part = slice(half * HB, (half + 1) * HB)
                nc.vector.reciprocal(inv_sums[:, :, part], sums[(N - 1) % 2][:, :, part]).then_inc(s_inv, 1)

            def add_out(g, c, bank=pp):
                dve.wait_ge(s_w0p, 2 * g + 1 + c)
                reach(dve, s_acc, 2 * g)
                a = acc[:].rearrange("p t e -> p (t e)")[:, bass.ds((g // PAIRS) * (QB * E) + c * 512, 512)]
                nc.vector.tensor_tensor(a, bank[:], a, ALU.add).then_inc(s_acc, 1)

            dve.wait_ge(s_w, 16 * W_DMAS)
            take_q(0, 0, False)
            take_q(0, 1, False, tp[0])
            for c in range(2):
                high_q(0, 0, c)
            for c in range(2):
                high_k(0, 0, c)
            dve.wait_ge(s_q_high, 1)
            nc.vector.tensor_tensor(q_low[0:D, :], q_raw[0:D, :], stacks[0][0:D, QA, :].bitcast(fp32),
                                    ALU.subtract).then_inc(s_cut, 1)
            nc.vector.tensor_tensor(q_low[D:P, :], q_raw[D:P, :], stacks[0][D:P, QBS, :].bitcast(fp32),
                                    ALU.subtract).then_inc(s_q_cut, 1)
            for c in range(2):
                take_v(0, 0, c, False, sc[1][:, c * 512:(c + 1) * 512])
            high_zt(0, x_high[:], xnt)
            dve.wait_ge(s_zt_high, 1)
            nc.vector.tensor_tensor(x_low[:], xnt[:], x_high[:].bitcast(fp32), ALU.subtract).then_inc(s_zt_cut, 1)
            high_w(1)

            def pair(g, parity, first, last, side):
                stage, c, after, before = side or (None, 0, False, False)
                for k in range(STEPS):
                    i, h = k // 2, k % 2
                    width = (QB - i) * P
                    dve.wait_ge(s_score, STEPS * g + k + 1)
                    nc.vector.tensor_reduce(neg_max[:, k:k + 1], sc[k % 2][:, 0:width], AX.X, ALU.max,
                                            negate=True).then_inc(s_max, 1)
                    if k == 0 and not first:
                        invert_sums(g - 1, 1 - parity)
                    if k in (0, 2) and not last:
                        take_q(g + 1, k // 2, True)
                    if k == 4 and not first:
                        add_out(g - 1, 0)
                    if k in (7, 8) and not last:
                        take_v(g + 1, 1 - parity, k - 7, not first, pp[:])
                    if k == 9 and not first:
                        add_out(g - 1, 1)
                    if k == 9 and last:
                        invert_half(0)
                    if k:
                        take_turn(g, k - 1)
                    if k in (1, 3) and not last:
                        high_q(g + 1, 1 - parity, k // 2)
                    if k in (5, 6) and not last:
                        high_k(g + 1, 1 - parity, k - 5)
                    if k == 14 and not last:
                        high_w(g + 2)
                    for wanted, table, b in ((after, AFTER, c - 1), (before, BEFORE, c + 1)):
                        if wanted and k in table.get(stage, {}):
                            for use in table[stage][k]:
                                use(b)

            pairs(dve, pair)
            take_turn(N - 1, STEPS - 1)
            invert_half(1)
            add_out(N - 1, 0)

            b = B - 1

            def add_half(dst, one, other, half):
                part = slice(half * HB, (half + 1) * HB)
                return nc.vector.tensor_tensor(dst[:, part, :], one[:, part, :], other[:, part, :], ALU.add)

            def first_norms(half, count):
                link(apply_to(2, res_b, acc_of(b), half, count), s_dt, b)
                link(add_half(x_b, x_b, res_b, half), s_dt, b)
                stats_of(3, x_b, half)

            dve.wait_ge(s_acc, 2 * N - 1)
            stats_of(2, acc_of(b), 0)
            dve.wait_ge(s_xb, 16 * B)
            first_norms(0, 5)
            add_out(N - 1, 1, tp[0])
            dve.wait_ge(s_acc, 2 * N)
            stats_of(2, acc_of(b), 1)
            apply_to(3, u_b, x_b, 0, 6).then_inc(s_u, 1)
            first_norms(1, 7)
            take_logits(b, tp[1])
            rank_logits(b)
            make_gate(b)
            apply_to(3, u_b, x_b, 1, 8).then_inc(s_u, 1)
            for half in range(2):
                take_up(b, half, (pp, tp[0])[half])
                dve.wait_ge(s_f, 2 * b + half + 1)
                stats_of(4, u_b, half)
            for half in range(2):
                link(apply_to(4, res_b, u_b, half, 9 + half), s_dt, b)
                add_half(res_b, res_b, x_b, half).then_inc(s_res, 1)


def kernel(**inputs):
    import numpy as np
    import concourse.bacc as bacc
    from concourse import mybir as mb
    from concourse.bass_utils import run_bass_kernel_spmd as run

    def a(name):
        return np.asarray(inputs[name])

    x = a("L0_attn_x")
    pairs = a("L0_attn_wq").shape[1] // 128

    def by_pair(w):
        return w.reshape(w.shape[0], pairs, 128).transpose(1, 0, 2)

    down, up = a("L0_ffn_lora_down"), a("L0_ffn_lora_up")
    arrays = {
        "x": x.reshape(-1, x.shape[-1]),
        "ln_gb": np.stack([a("L0_attn_ln_g"), a("L0_attn_ln_b")], axis=1),
        "w_pairs": np.concatenate([by_pair(a(f"L0_attn_w{c}")) for c in "qkv"], axis=2),
        "qk_bias": np.stack([a("L0_attn_bq").reshape(pairs, 128), a("L0_attn_bk").reshape(pairs, 128)], axis=2),
        "bv": a("L0_attn_bv").reshape(1, -1),
        "w0": a("L0_attn_w0"),
        "b0": a("L0_attn_b0").reshape(1, -1),
        "router_t": a("L0_ffn_router_w").T,
        "down_t": down.reshape(-1, down.shape[-1]).T,
        "up_r": up.transpose(0, 2, 1).reshape(-1, up.shape[1]),
    }
    arrays = {n: np.ascontiguousarray(v) for n, v in arrays.items()}
    nc = bacc.Bacc("TRN2", target_bir_lowering=False, num_devices=1)
    f32 = mb.dt.float32
    args = {n: nc.dram_tensor(n, v.shape, mb.dt.from_np(v.dtype), kind="ExternalInput").ap() for n, v in arrays.items()}
    out = nc.dram_tensor("out", arrays["x"].shape, f32, kind="ExternalOutput").ap()
    sums = nc.dram_tensor("sums_dram", (2, 128, 8), f32).ap()
    sandwich_kernel(nc, out=out, sums_dram=sums, **args)
    r = run(nc, [arrays], core_ids=[0])
    return r.results[0]["out"].reshape(x.shape)
```
